# Optimizing a Trainium2 kernel written in Bass

```python
import numpy as np
import jax
import jax.numpy as jnp

def _softmax(x, axis=-1):
    return jax.nn.softmax(x, axis=axis)

def _gelu(x):
    return jax.nn.gelu(x, approximate=True)

def _silu(x):
    return jax.nn.silu(x)

def _sigmoid(x):
    return jax.nn.sigmoid(x)

def _layernorm(x, axis=-1, eps=1e-05):
    m = jnp.mean(x, axis=axis, keepdims=True)
    v = jnp.var(x, axis=axis, keepdims=True)
    return (x - m) / jnp.sqrt(v + eps)

def _scatter_add(tgt, idx, src, axis=0):
    return tgt.at[idx].add(src)

def _segment_sum(src, seg, n):
    return jax.ops.segment_sum(src, seg, n)
kernel_name = 'mk_flamingo_gated_d1_seqx_r4_ac154b'

def setup_inputs(seed: int=0):
    np.random.seed(seed)
    _w = jnp.asarray

    def _rec_inputs():
        import jax
        import jax.numpy as jnp
        _rk = jax.random.key(seed)
        x = -0.0002928 + 1 * jax.random.normal(jax.random.fold_in(_rk, 1), (8, 256, 256), jnp.float32)
        _lenS = 256 - jax.random.randint(jax.random.fold_in(_rk, 7), (8,), 0, max(1, 256 // 4) + 1, jnp.int32)
        _lenS2 = 77 - jax.random.randint(jax.random.fold_in(_rk, 8), (8,), 0, max(1, 77 // 4) + 1, jnp.int32)
        _ctx_1024P = jax.random.normal(jax.random.fold_in(_rk, 11), (8, 16, 256), jnp.float32)
        _ctx_1024c = jax.random.dirichlet(jax.random.fold_in(_rk, 511), 0.3 * jnp.ones((16,), jnp.float32), (8, 77))
        _ctx_1024t = jnp.einsum('bsk,bkd->bsd', _ctx_1024c, _ctx_1024P)
        _ctx_1024t = _ctx_1024t * jax.lax.rsqrt(jnp.mean(jnp.square(_ctx_1024t)) + 1e-12) * 0.953939
        ctx_1024 = -1.39393e-06 + 0.999914 * (_ctx_1024t + 0.3 * jax.random.normal(jax.random.fold_in(_rk, 611), (8, 77, 256), jnp.float32))
        _validS = jnp.arange(256)[None, :] < _lenS[:, None]
        _validS2 = jnp.arange(77)[None, :] < _lenS2[:, None]
        _causal = jnp.tril(jnp.ones((256, 256), dtype=bool))
        mask_Bx1xSxS2_ff1 = jnp.where(jnp.ones((8, 1, 256, 77), dtype=bool), 1.0, 0.0).astype(jnp.float32)
        _g = jax.random.normal(jax.random.fold_in(_rk, 9001), (2, 1), jnp.float32)
        _g = jnp.sign(_g) * jnp.maximum(jnp.abs(_g), 1.0) + (_g == 0) * 1.0
        g_xattn = _g[0]
        g_ffn = _g[1]
        return (x, ctx_1024, mask_Bx1xSxS2_ff1, g_xattn, g_ffn)
    x, ctx_1024, mask_Bx1xSxS2_ff1, g_xattn, g_ffn = _rec_inputs()

    def _L0_xattn_setup():
        import jax, jax.numpy as jnp
        import numpy as np
        MODEL_SIZE = 256
        H = 16
        KEY_SIZE = MODEL_SIZE // H
        B, LQ, LK = (2, 512, 512)
        NEG_INF = -1000000000.0
        key = jax.random.key(seed)
        ks = jax.random.split(key, 10)
        s = 0.02
        return {'decoder_output': jax.random.normal(ks[0], (B, LQ, MODEL_SIZE), dtype=jnp.float32), 'encoder_output': jax.random.normal(ks[1], (B, LK, MODEL_SIZE), dtype=jnp.float32), 'mask': jnp.ones((B, 1, LQ, LK), dtype=jnp.float32), 'wq_w': jax.random.normal(ks[2], (MODEL_SIZE, MODEL_SIZE), dtype=jnp.float32) * s, 'wq_b': jnp.zeros((MODEL_SIZE,), dtype=jnp.float32), 'wk_w': jax.random.normal(ks[3], (MODEL_SIZE, MODEL_SIZE), dtype=jnp.float32) * s, 'wk_b': jnp.zeros((MODEL_SIZE,), dtype=jnp.float32), 'wv_w': jax.random.normal(ks[4], (MODEL_SIZE, MODEL_SIZE), dtype=jnp.float32) * s, 'wv_b': jnp.zeros((MODEL_SIZE,), dtype=jnp.float32), 'wo_w': jax.random.normal(ks[5], (MODEL_SIZE, MODEL_SIZE), dtype=jnp.float32) * s, 'wo_b': jnp.zeros((MODEL_SIZE,), dtype=jnp.float32)}
    _L0_xattn_all = _L0_xattn_setup()
    _L0_xattn_in = {k: v for k, v in _L0_xattn_all.items() if k in ('wq_w', 'wq_b', 'wk_w', 'wk_b', 'wv_w', 'wv_b', 'wo_w', 'wo_b')}
    del _L0_xattn_all

    def _L0_ffn_setup():
        import jax, jax.numpy as jnp
        import numpy as np
        B, S, D, F, E, K = (4, 512, 256, 1024, 4, 2)
        key = jax.random.key(seed)
        k = jax.random.split(key, 6)
        x = jax.random.normal(k[0], (B, S, D), jnp.float32)
        router_w = jax.random.normal(k[1], (D, E), jnp.float32) * D ** (-0.5)
        router_b = jnp.zeros((E,), jnp.float32)
        w1 = jax.random.normal(k[2], (E, D, F), jnp.float32) * 0.02
        w3 = jax.random.normal(k[3], (E, D, F), jnp.float32) * 0.02
        w2 = jax.random.normal(k[4], (E, F, D), jnp.float32) * 0.02
        return {'x': x, 'router_w': router_w, 'router_b': router_b, 'w1': w1, 'w3': w3, 'w2': w2}
    _L0_ffn_all = _L0_ffn_setup()
    _L0_ffn_in = {k: v for k, v in _L0_ffn_all.items() if k in ('router_w', 'router_b', 'w1', 'w3', 'w2')}
    del _L0_ffn_all
    return {'x': x, 'ctx_1024': ctx_1024, 'mask_Bx1xSxS2_ff1': mask_Bx1xSxS2_ff1, 'g_xattn': g_xattn, 'g_ffn': g_ffn, 'L0_xattn_wq_w': _L0_xattn_in['wq_w'], 'L0_xattn_wq_b': _L0_xattn_in['wq_b'], 'L0_xattn_wk_w': _L0_xattn_in['wk_w'], 'L0_xattn_wk_b': _L0_xattn_in['wk_b'], 'L0_xattn_wv_w': _L0_xattn_in['wv_w'], 'L0_xattn_wv_b': _L0_xattn_in['wv_b'], 'L0_xattn_wo_w': _L0_xattn_in['wo_w'], 'L0_xattn_wo_b': _L0_xattn_in['wo_b'], 'L0_ffn_router_w': _L0_ffn_in['router_w'], 'L0_ffn_router_b': _L0_ffn_in['router_b'], 'L0_ffn_w1': _L0_ffn_in['w1'], 'L0_ffn_w3': _L0_ffn_in['w3'], 'L0_ffn_w2': _L0_ffn_in['w2']}

def reference(x, ctx_1024, mask_Bx1xSxS2_ff1, g_xattn, g_ffn, L0_xattn_wq_w, L0_xattn_wq_b, L0_xattn_wk_w, L0_xattn_wk_b, L0_xattn_wv_w, L0_xattn_wv_b, L0_xattn_wo_w, L0_xattn_wo_b, L0_ffn_router_w, L0_ffn_router_b, L0_ffn_w1, L0_ffn_w3, L0_ffn_w2):
    import jax
    import jax.numpy as jnp

    def _L0_xattn_ref(decoder_output, encoder_output, mask, wq_w, wq_b, wk_w, wk_b, wv_w, wv_b, wo_w, wo_b):
        import jax, jax.numpy as jnp
        import numpy as np
        MODEL_SIZE = 256
        H = 16
        KEY_SIZE = MODEL_SIZE // H
        B, LQ, LK = (2, 512, 512)
        NEG_INF = -1000000000.0
        b = decoder_output.shape[0]
        q = decoder_output @ wq_w + wq_b
        k = encoder_output @ wk_w + wk_b
        v = encoder_output @ wv_w + wv_b
        q = q.reshape(b, -1, H, KEY_SIZE).transpose(0, 2, 1, 3)
        k = k.reshape(b, -1, H, KEY_SIZE).transpose(0, 2, 1, 3)
        v = v.reshape(b, -1, H, KEY_SIZE).transpose(0, 2, 1, 3)
        score = jnp.einsum('bhqd,bhkd->bhqk', q, k) / jnp.sqrt(jnp.asarray(KEY_SIZE, dtype=jnp.float32))
        score = score * mask
        score = jnp.where(score == 0, jnp.float32(NEG_INF), score)
        alignment = jax.nn.softmax(score, axis=-1)
        context = jnp.einsum('bhqk,bhkd->bhqd', alignment, v)
        context = context.transpose(0, 2, 1, 3).reshape(b, -1, H * KEY_SIZE)
        heads = context @ wo_w + wo_b
        return heads

    def _L0_ffn_ref(x, router_w, router_b, w1, w3, w2):
        import jax, jax.numpy as jnp
        import numpy as np
        B, S, D, F, E, K = (4, 512, 256, 1024, 4, 2)
        b, s, d = x.shape
        T = b * s
        e = router_w.shape[1]
        xf = x.reshape(T, d)
        logits = xf @ router_w + router_b
        probs = jax.nn.softmax(logits, axis=-1)
        top_p, top_i = jax.lax.top_k(probs, K)
        top_p = top_p / jnp.sum(top_p, axis=-1, keepdims=True)
        gates = jnp.zeros((T, e), xf.dtype).at[jnp.arange(T)[:, None], top_i].add(top_p)
        h = jax.nn.silu(jnp.einsum('td,edf->etf', xf, w1)) * jnp.einsum('td,edf->etf', xf, w3)
        expert_out = jnp.einsum('etf,efd->etd', h, w2)
        out = jnp.einsum('te,etd->td', gates, expert_out)
        return out.reshape(b, s, d)
    x = x + jnp.tanh(g_xattn[0]) * _L0_xattn_ref(_layernorm(x, axis=-1), ctx_1024, mask_Bx1xSxS2_ff1, L0_xattn_wq_w, L0_xattn_wq_b, L0_xattn_wk_w, L0_xattn_wk_b, L0_xattn_wv_w, L0_xattn_wv_b, L0_xattn_wo_w, L0_xattn_wo_b)
    x = x + jnp.tanh(g_ffn[0]) * _L0_ffn_ref(_layernorm(x, axis=-1), L0_ffn_router_w, L0_ffn_router_b, L0_ffn_w1, L0_ffn_w3, L0_ffn_w2)
    return x

_drawn_inputs = setup_inputs


def setup_inputs(seed=0):
    import zlib

    import numpy as np

    out = dict(_drawn_inputs(seed))
    spreads = {'L0_xattn_wq_b': (0.0, 0.8),
     'L0_xattn_wk_b': (0.0, 0.8),
     'L0_xattn_wv_b': (0.0, 0.303),
     'L0_xattn_wo_b': (0.0, 0.1),
     'L0_ffn_router_b': (0.0, 0.8)}
    factors = {'L0_xattn_wq_w': 8.0, 'L0_xattn_wk_w': 8.0, 'L0_ffn_router_w': 3.033}
    for name, (base, spread) in spreads.items():
        noise = np.random.default_rng([zlib.crc32(name.encode()), seed]).standard_normal(out[name].shape)
        drawn = base * np.exp(spread * noise) if base else spread * noise
        out[name] = jnp.asarray(drawn.astype(out[name].dtype))
    for name, factor in factors.items():
        out[name] = (out[name] * factor).astype(out[name].dtype)
    return out
```

```python
from contextlib import ExitStack

import numpy as np

import concourse.bass as bass
from concourse import mybir
from concourse.alu_op_type import AluOpType as ALU

ACT = mybir.ActivationFunctionType
F32 = mybir.dt.float32
F32R = mybir.dt.float32r
AX = mybir.AxisListType

P = 128
B, SQ, D = 8, 256, 256
SK = 77
H, DH = 16, 16
E, F = 4, 1024
T = B * SQ
NT = T // P
QT = SQ // P
DC = D // P
HG = H // DC
GK = HG * SK
BK = 4 * SK
NC = -(-GK // P)
ROWS = [min(P, GK - c * P) for c in range(NC)]
HEAD0 = [c * P // SK for c in range(NC)]
WIDTH = [((c * P + ROWS[c] - 1) // SK - HEAD0[c] + 1) * DH for c in range(NC)]
VW = 48
NS = 2 * QT
FC = F // P
TC = 512
NTC = T // TC
MASKED = -1e9 * 4.0
EPS = 1e-5


def constants():
    row = np.arange(NC * P)
    ident = np.eye(P, dtype=np.float32)
    head_rows = (np.arange(P)[:, None] // DH == np.arange(HG)[None]).astype(np.float32)
    owner = (row[:, None] // SK == np.arange(P)[None] // DH).astype(np.float32)
    owner = owner.reshape(NC, P, P).transpose(1, 0, 2).reshape(P, NC * P)
    spread = (row[None] % SK == np.arange(SK)[:, None]).astype(np.float32)
    tie = (np.arange(E)[None, :] < np.arange(E)[:, None]).astype(np.float32).reshape(1, E * E)
    tie = np.repeat(tie, P, 0)
    return {"ident": ident, "head_rows": head_rows, "owner": np.ascontiguousarray(owner), "spread": spread, "tie": tie}


def flamingo_block(nc, x, ctx_in, mask, g_xattn, g_ffn, wq, bq, wk, bk, wv, bv, wo, bo,
                   rw, rb, w1, w3, w2, ident_in, head_rows_in, owner_in, spread_in, tie_in, out):
    with ExitStack() as keep:
        def sb(name, shape, dt=F32, stack=keep):
            return stack.enter_context(nc.sbuf_tensor(name, shape, dt))

        def sem(name):
            return keep.enter_context(nc.semaphore(name))

        xall = sb("xall", [P, NT, D])
        logits = sb("logits", [P, NT, E])
        gates = sb("gates", [P, NT, E])
        xt_hi = sb("xt_hi", [P, DC, T], F32R)
        xt_lo = sb("xt_lo", [P, DC, T], F32R)
        wa_hi = sb("wa_hi", [P, 3, 2048], F32R)
        wa_lo = sb("wa_lo", [P, 3, 2048], F32R)
        stage = sb("stage", [P, 2048])
        tanh_g = sb("tanh_g", [P, 2])
        gate_in = sb("gate_in", [P, 2])
        rbias = sb("rbias", [P, E])
        tie = sb("tie", [P, E, E])

        att = ExitStack()
        maskt = sb("maskt", [P, NT, SK], stack=att)
        ctxs = sb("ctxs", [SK, B, D], stack=att)
        ctxT = sb("ctxT", [P, DC, B * SK], stack=att)
        kT = sb("kT", [P, DC, B * SK], stack=att)
        vals = sb("vals", [SK, B, D], stack=att)
        wqs = sb("wqs", [P, DC, D], stack=att)
        wks = sb("wks", [P, DC, D], stack=att)
        wvs = sb("wvs", [P, DC, D], stack=att)
        wos = sb("wos", [P, DC, D], stack=att)
        rws = sb("rws", [P, DC, E], stack=att)
        bqs = sb("bqs", [P, DC], stack=att)
        bks = sb("bks", [P, DC], stack=att)
        bvs = sb("bvs", [P, D], stack=att)
        bos = sb("bos", [P, D], stack=att)
        ident = sb("ident", [P, P], stack=att)
        head_rows = sb("head_rows", [P, HG], stack=att)
        owner = sb("owner", [P, NC, P], stack=att)
        spread = sb("spread", [SK, NC * P], stack=att)
        half = sb("half", [P, NT], stack=att)
        stats1 = sb("stats1", [P, NT, 6], stack=att)
        mv1 = sb("mv1", [P, NT, 2], stack=att)
        vareps1 = sb("vareps1", [P, NT], stack=att)
        rstd1 = sb("rstd1", [P, NT], stack=att)
        stats = sb("stats", [P, QT, 6], stack=att)
        mv = sb("mv", [P, QT, 2], stack=att)
        vareps = sb("vareps", [P, QT], stack=att)
        rstd = sb("rstd", [P, QT], stack=att)
        xn = sb("xn", [P, QT, D], stack=att)
        xn2 = sb("xn2", [P, QT, D], stack=att)
        xnT = sb("xnT", [P, DC, SQ], stack=att)
        xn2T = sb("xn2T", [P, DC, SQ], stack=att)
        qT = sb("qT", [P, DC, SQ], stack=att)
        kblock = sb("kblock", [P, DC, HG, SK], stack=att)
        vblock = sb("vblock", [P, NC, DC, P], stack=att)
        score = sb("score", [P, 2, HG, SK], stack=att)
        zero_at = sb("zero_at", [P, HG, SK], stack=att)
        top = sb("top", [P, HG], stack=att)
        prob = sb("prob", [P, 2, HG * SK], stack=att)
        probT = sb("probT", [P, DC, NC, SQ], stack=att)
        rden = sb("rden", [P, SQ], stack=att)
        ctxn = sb("ctxn", [P, DC, SQ], stack=att)

        ps_scores = [att.enter_context(nc.psum_tensor(f"ps_scores{i}", [P, 2, 512], F32)) for i in range(2)]
        ps_probT = att.enter_context(nc.psum_tensor("ps_probT", [P, 2, 512], F32))
        ps_av = att.enter_context(nc.psum_tensor("ps_av", [P, 2, SQ], F32))
        ps_misc = att.enter_context(nc.psum_tensor("ps_misc", [P, 512], F32))

        ld_first = sem("ld_first")
        ld_ctx = sem("ld_ctx")
        ld_rest = sem("ld_rest")
        cleared = sem("cleared")
        ctx_turned, ctx_copied = sem("ctx_turned"), sem("ctx_copied")
        keys_done, keys_copied = sem("keys_done"), sem("keys_copied")
        vals_done, vals_copied = sem("vals_done"), sem("vals_copied")
        bo_ready = sem("bo_ready")
        tanh_done = sem("tanh_done")
        stat_step, aggr_step, stat_done, rstd_done, norm_done = sem("stat_step"), sem("aggr_step"), sem("stat_done"), sem("rstd_done"), sem("norm_done")
        stat2_step, aggr2_step, stat2_done, rstd2_done, norm2_done = sem("stat2_step"), sem("aggr2_step"), sem("stat2_done"), sem("rstd2_done"), sem("norm2_done")
        xT_done, xT_copied = sem("xT_done"), sem("xT_copied")
        q_done, q_copied = sem("q_done"), sem("q_copied")
        kblock_done = sem("kblock_done")
        vspread_done, vblock_done = sem("vspread_done"), sem("vblock_done")
        biased = sem("biased")
        scores_done, masked, soft_step, shifted = sem("scores_done"), sem("masked"), sem("soft_step"), sem("shifted")
        exp_done, turned, turned_copied = sem("exp_done"), sem("turned"), sem("turned_copied")
        av_done, rden_done, av_copied = sem("av_done"), sem("rden_done"), sem("av_copied")
        wo_done, x2_done = sem("wo_done"), sem("x2_done")
        x2T_done, x2T_copied = sem("x2T_done"), sem("x2T_copied")
        xhi_done, xlo_done = sem("xhi_done"), sem("xlo_done")
        lg_done, lg_copied = sem("lg_done"), sem("lg_copied")
        staged, w_hi_done, w_lo_done = sem("staged"), sem("w_hi_done"), sem("w_lo_done")
        out_written = sem("out_written")

        def wide(ap, n):
            return ap.unsqueeze(1).to_broadcast([ap.shape[0], n, ap.shape[1]])

        with nc.Block() as block:
            @block.sync
            def _(sp):
                for dst, src in ((xall[:, 0:QT, :], x[0:1].rearrange("b (t p) d -> p (b t) d", p=P)),
                                 (ident[:], ident_in)):
                    sp.dma_start(dst, src).then_inc(ld_first, 16)
                for dst, src in ((ctxs[:], ctx_in.rearrange("b k d -> k b d")),
                                 (wks[:], wk.rearrange("(c p) n -> p c n", p=P)),
                                 (wvs[:], wv.rearrange("(c p) n -> p c n", p=P))):
                    sp.dma_start(dst, src).then_inc(ld_ctx, 16)
                for dst, src in ((maskt[:], mask.rearrange("b o (t p) k -> p (b o t) k", p=P)),
                                 (xall[:, QT:, :], x[1:].rearrange("b (t p) d -> p (b t) d", p=P)),
                                 (wqs[:], wq.rearrange("(c p) n -> p c n", p=P)),
                                 (wos[:], wo.rearrange("(c p) n -> p c n", p=P)),
                                 (rws[:], rw.rearrange("(c p) n -> p c n", p=P))):
                    sp.dma_start(dst, src).then_inc(ld_rest, 16)
                for m in range(3):
                    if m:
                        sp.wait_ge(w_lo_done, m)
                    src = (w1, w3, w2)[m][0].rearrange("(c p) n -> p c n", p=P)
                    sp.dma_start(stage[:].rearrange("p (c n) -> p c n", c=src.shape[1]), src).then_inc(staged, 16)

            @block.scalar
            def _(act):
                act.dma_start(owner[:], owner_in.rearrange("p (c n) -> p c n", c=NC)).then_inc(ld_ctx, 16)
                act.dma_start(spread[:], spread_in).then_inc(ld_ctx, 16)
                act.dma_start(head_rows[:], head_rows_in).then_inc(ld_ctx, 16)
                with nc.allow_non_contiguous_dma(reason="biases laid along the partitions"):
                    act.dma_start(bqs[:], bq.rearrange("(c p) -> p c", p=P)).then_inc(ld_ctx, 16)
                    act.dma_start(bks[:], bk.rearrange("(c p) -> p c", p=P)).then_inc(ld_ctx, 16)
                for dst, src in ((bvs[:], bv), (bos[:], bo), (rbias[:], rb), (gate_in[:, 0:1], g_xattn), (gate_in[:, 1:2], g_ffn)):
                    act.dma_start(dst, src.unsqueeze(0).to_broadcast([P, src.shape[0]])).then_inc(ld_ctx, 16)
                act.dma_start(tie[:], tie_in.rearrange("p (i j) -> p i j", i=E)).then_inc(ld_ctx, 16)
                act.wait_ge(ld_ctx, LD_CTX)
                act.activation(tanh_g[:], gate_in[:], ACT.Tanh).then_inc(tanh_done, 1)

                for g in range(DC):
                    act.wait_ge(keys_done, g + 1)
                    act.activation(kT[:, g, :].rearrange("p (h n) -> p h n", h=2), ps_scores[g][:, :, 0:4 * SK],
                                   ACT.Identity, bias=bks[:, g:g + 1]).then_inc(keys_copied, 1)

                def xT_copy(b):
                    act.wait_ge(xT_done, b + 1)
                    act.copy(xnT[:].rearrange("p c n -> p (c n)"), ps_misc[:]).then_inc(xT_copied, 1)

                def q_copy(b):
                    act.wait_ge(q_done, b + 1)
                    act.activation(qT[:, 0, :], ps_misc[:, 0:SQ], ACT.Identity, bias=bqs[:, 0:1]).then_inc(q_copied, 1)
                    act.activation(qT[:, 1, :], ps_misc[:, SQ:], ACT.Identity, bias=bqs[:, 1:2]).then_inc(q_copied, 1)

                def exponent(b, s, first):
                    act.wait_ge(shifted, NS * b + s + 1)
                    if not (first and s < 2):
                        act.wait_ge(turned, NS * b + s - 1)
                    act.activation(prob[:, s % 2, :], score[:, s % 2].rearrange("p h k -> p (h k)"), ACT.Exp,
                                   scale=0.25).then_inc(exp_done, 1)

                def probT_copy(b, s, first):
                    g, t = s // QT, s % QT
                    act.wait_ge(turned, NS * b + s + 1)
                    if not first:
                        act.wait_ge(av_done, 2 * b + g - 1)
                    act.copy(probT[:, g, 0:4, t * P:(t + 1) * P],
                             ps_probT[:, 0, :].rearrange("p (c n) -> p c n", c=4)).then_inc(turned_copied, 1)
                    act.copy(probT[0:ROWS[4], g, 4, t * P:(t + 1) * P], ps_probT[0:ROWS[4], 1, 0:P]).then_inc(turned_copied, 1)

                def x2T_copy(b, first):
                    act.wait_ge(x2T_done, b + 1)
                    if not first:
                        act.wait_ge(xlo_done, b)
                        act.wait_ge(lg_done, b)
                    act.copy(xn2T[:].rearrange("p c n -> p (c n)"), ps_misc[:]).then_inc(x2T_copied, 1)
                    act.wait_ge(x2T_copied, b + 1)
                    act.copy(xt_hi[:, :, bass.ds(b * SQ, SQ)], xn2T[:]).then_inc(xhi_done, 1)

                def body(b, first=False, last=False):
                    exponent(b, 0, first)
                    if not first:
                        x2T_copy(b - 1, isinstance(b, int) and b == 1)
                    exponent(b, 1, first)
                    probT_copy(b, 0, first)
                    exponent(b, 2, first)
                    if not last:
                        xT_copy(b + 1)
                    probT_copy(b, 1, first)
                    exponent(b, 3, first)
                    if not last:
                        q_copy(b + 1)
                    probT_copy(b, 2, first)
                    probT_copy(b, 3, first)

                xT_copy(0)
                q_copy(0)
                body(0, first=True)
                body(1)
                for m in range(3):
                    act.wait_ge(staged, 16 * (m + 1))
                    act.copy(wa_hi[:, m], stage[:]).then_inc(w_hi_done, 1)
                with act.Fori(2, B - 1) as b:
                    body(b)
                body(B - 1, last=True)
                x2T_copy(B - 1, False)

            @block.gpsimd
            def _(pool):
                pool.memset(half[:], -0.5).then_inc(cleared, 1)
                pool.memset(vblock[:], 0.0).then_inc(cleared, 1)

                def rsqrt(i, t0, t1):
                    pool.wait_ge(stat_done, i + 1)
                    pool.tensor_tensor(rstd1[:, t0:t1], vareps1[:, t0:t1], half[:, t0:t1], ALU.pow).then_inc(rstd_done, 1)

                def rsqrt2(b):
                    pool.wait_ge(stat2_done, b + 1)
                    if not (isinstance(b, int) and b == 0):
                        pool.wait_ge(norm2_done, 2 * b)
                    pool.tensor_tensor(rstd[:], vareps[:], half[:, 0:QT], ALU.pow).then_inc(rstd2_done, 1)

                def keys(b, g):
                    if not (isinstance(b, int) and b == 0):
                        pool.wait_ge(scores_done, NS * (b - 1) + QT * (g + 1))
                    pool.tensor_tensor(kblock[:, g], wide(kT[:, g, bass.ds(b * SK, SK)], HG),
                                       head_rows[:].unsqueeze(2).to_broadcast([P, HG, SK]), ALU.mult).then_inc(kblock_done, 1)

                def bias_add(b):
                    pool.wait_ge(norm_done, 2 * b + 2)
                    pool.tensor_tensor(xall[:, bass.ds(b * QT, QT), :], xall[:, bass.ds(b * QT, QT), :], wide(bos[:], QT),
                                       ALU.add).then_inc(biased, 1)

                def body(b, first=False, last=False):
                    if not first:
                        rsqrt2(b - 1)
                    if not last:
                        keys(b + 1, 0)
                        bias_add(b + 1)
                        keys(b + 1, 1)

                pool.wait_ge(cleared, 1)
                rsqrt(0, 0, QT)
                pool.wait_ge(keys_copied, 2)
                keys(0, 0)
                keys(0, 1)
                pool.wait_ge(tanh_done, 1)
                pool.tensor_scalar(bos[:], bos[:], tanh_g[:, 0:1], 0.0, ALU.mult, ALU.add).then_inc(bo_ready, 1)
                pool.wait_ge(bo_ready, 1)
                bias_add(0)
                rsqrt(1, QT, NT)
                body(0, first=True)
                body(1)
                for m in range(3):
                    pool.wait_ge(w_hi_done, m + 1)
                    pool.tensor_tensor(wa_lo[:, m], stage[:], wa_hi[:, m].bitcast(F32), ALU.subtract).then_inc(w_lo_done, 1)
                with pool.Fori(2, B - 1) as b:
                    body(b)
                body(B - 1, last=True)
                rsqrt2(B - 1)

            @block.vector
            def _(dve):
                def wait_apart(signal, value):
                    dve.wait_ge(ld_first, 16 * 2)
                    dve.wait_ge(signal, value)

                def stats_of_x(t0, t1):
                    for t in range(t0, t1):
                        dve.bn_stats(stats1[:, t], xall[:, t]).then_inc(stat_step, 1)
                    dve.wait_ge(stat_step, t1)
                    for t in range(t0, t1):
                        dve.bn_aggr(mv1[:, t], stats1[:, t]).then_inc(aggr_step, 1)
                    dve.wait_ge(aggr_step, t1)
                    dve.tensor_scalar(vareps1[:, t0:t1], mv1[:, t0:t1, 1], EPS, None, ALU.add).then_inc(stat_done, 1)

                def norm(b):
                    if isinstance(b, int) and b < 2:
                        dve.wait_ge(rstd_done, b + 1)
                    if not (isinstance(b, int) and b == 0):
                        dve.wait_ge(xT_done, b)
                    for t in range(QT):
                        dve.tensor_scalar(xn[:, t], xall[:, bass.ds(b * QT + t, 1), :].rearrange("p o d -> p (o d)"),
                                          mv1[:, bass.ds(b * QT + t, 1), 0], rstd1[:, bass.ds(b * QT + t, 1)], ALU.subtract, ALU.mult).then_inc(norm_done, 1)

                def residual(b):
                    dve.wait_ge(wo_done, b + 1)
                    dve.wait_ge(biased, b + 1)
                    dve.scalar_tensor_tensor(out=xall[:, bass.ds(b * QT, QT), :], in0=ps_misc[:].rearrange("p (t d) -> p t d", t=QT),
                                             scalar=tanh_g[:, 0:1], in1=xall[:, bass.ds(b * QT, QT), :],
                                             op0=ALU.mult, op1=ALU.add).then_inc(x2_done, 1)

                def stat2(b):
                    wait_apart(x2_done, b + 1)
                    for t in range(QT):
                        st = dve.bn_stats(stats[:, t], xall[:, bass.ds(b * QT + t, 1), :].rearrange("p o d -> p (o d)"))
                    st.then_inc(stat2_step, 1)
                    wait_apart(stat2_step, b + 1)
                    for t in range(QT):
                        st = dve.bn_aggr(mv[:, t], stats[:, t])
                    st.then_inc(aggr2_step, 1)
                    dve.wait_ge(aggr2_step, b + 1)
                    if not (isinstance(b, int) and b == 0):
                        dve.wait_ge(rstd2_done, b)
                    dve.tensor_scalar(vareps[:], mv[:, :, 1], EPS, None, ALU.add).then_inc(stat2_done, 1)

                def norm2(b):
                    dve.wait_ge(rstd2_done, b + 1)
                    if not (isinstance(b, int) and b == 0):
                        dve.wait_ge(x2T_done, b)
                    for t in range(QT):
                        dve.tensor_scalar(xn2[:, t], xall[:, bass.ds(b * QT + t, 1), :].rearrange("p o d -> p (o d)"),
                                          mv[:, t, 0:1], rstd[:, t:t + 1], ALU.subtract, ALU.mult).then_inc(norm2_done, 1)

                def softmax(b, s, first):
                    n = NS * b + s
                    t = s % QT
                    sc = score[:, s % 2]
                    dve.wait_ge(scores_done, n + 1)
                    if not (first and s < 2):
                        dve.wait_ge(exp_done, n - 1)
                    mk = maskt[:, bass.ds(b * QT + t, 1), :].to_broadcast([P, 4, SK])
                    for h in range(2):
                        dve.tensor_tensor(sc[:, 4 * h:4 * h + 4], ps_scores[s % 2][:, h, 0:BK].rearrange("p (h k) -> p h k", h=4), mk,
                                          ALU.mult).then_inc(masked, 1)
                    dve.wait_ge(masked, 2 * n + 2)
                    dve.tensor_scalar(zero_at[:], sc, 0.0, MASKED, ALU.is_equal, ALU.mult).then_inc(soft_step, 1)
                    dve.wait_ge(soft_step, 3 * n + 1)
                    dve.tensor_tensor(sc, sc, zero_at[:], ALU.add).then_inc(soft_step, 1)
                    dve.wait_ge(soft_step, 3 * n + 2)
                    dve.tensor_reduce(top[:], sc, AX.X, ALU.max).then_inc(soft_step, 1)
                    dve.wait_ge(soft_step, 3 * n + 3)
                    dve.tensor_tensor(sc, sc, top[:].unsqueeze(2).to_broadcast([P, HG, SK]), ALU.subtract).then_inc(shifted, 1)

                def context(b, g, first):
                    dve.wait_ge(av_done, 2 * b + g + 1)
                    if not (first and g == 0):
                        dve.wait_ge(av_copied, 2 * b + g)
                    dve.reciprocal(rden[:], ps_av[:, 1, :]).then_inc(rden_done, 1)
                    dve.wait_ge(rden_done, 2 * b + g + 1)
                    if not first:
                        dve.wait_ge(wo_done, b)
                    dve.tensor_tensor(ctxn[:, g, :], ps_av[:, 0, :], rden[:], ALU.mult).then_inc(av_copied, 1)

                def values(b):
                    dve.wait_ge(vspread_done, b + 1)
                    for c in range(NC):
                        cols = slice(HEAD0[c] * DH, HEAD0[c] * DH + WIDTH[c])
                        dve.tensor_tensor(vblock[0:ROWS[c], c, :, cols],
                                          ps_misc[0:ROWS[c], c * 2 * VW:(c + 1) * 2 * VW].rearrange("p (g n) -> p g n", g=DC)[:, :, 0:WIDTH[c]],
                                          wide(owner[0:ROWS[c], c, cols], DC), ALU.mult).then_inc(vblock_done, 1)

                def split2(b):
                    dve.wait_ge(xhi_done, b + 1)
                    dve.tensor_tensor(xt_lo[:, :, bass.ds(b * SQ, SQ)], xn2T[:], xt_hi[:, :, bass.ds(b * SQ, SQ)].bitcast(F32),
                                      ALU.subtract).then_inc(xlo_done, 1)

                def logit(b):
                    dve.wait_ge(lg_done, b + 1)
                    dve.tensor_tensor(logits[:, bass.ds(b * QT, QT), :], ps_misc[:, 0:QT * E].rearrange("p (t e) -> p t e", t=QT),
                                      wide(rbias[:], QT), ALU.add).then_inc(lg_copied, 1)

                def body(b, first=False, last=False):
                    softmax(b, 0, first)
                    if not first:
                        residual(b - 1)
                        stat2(b - 1)
                    softmax(b, 1, first)
                    if not first:
                        norm2(b - 1)
                    if not last:
                        norm(b + 1)
                    softmax(b, 2, first)
                    if not first:
                        split2(b - 1)
                        logit(b - 1)
                    softmax(b, 3, first)
                    context(b, 0, first)
                    context(b, 1, first)
                    if not last:
                        values(b + 1)

                dve.wait_ge(ld_first, 16 * 2)
                stats_of_x(0, QT)
                for c in range(DC):
                    dve.wait_ge(ctx_turned, c + 1)
                    dve.tensor_copy(ctxT[:, c, :].rearrange("p (h n) -> p h n", h=2), ps_scores[c][:, :, 0:4 * SK]).then_inc(ctx_copied, 1)
                norm(0)
                for i in range(2):
                    dve.wait_ge(vals_done, i + 1)
                    dve.tensor_tensor(vals[:, 4 * i:4 * i + 4, :], ps_scores[i][0:SK].rearrange("p h (b n) -> p (h b) n", b=2),
                                      wide(bvs[0:SK, :], 4), ALU.add).then_inc(vals_copied, 1)
                dve.wait_ge(cleared, 2)
                values(0)
                dve.wait_ge(tanh_done, 1)
                dve.wait_ge(ld_rest, 16 * 5)
                stats_of_x(QT, NT)
                body(0, first=True)
                with dve.Fori(1, B - 1) as b:
                    body(b)
                body(B - 1, last=True)
                residual(B - 1)
                stat2(B - 1)
                norm2(B - 1)
                split2(B - 1)
                logit(B - 1)

            @block.tensor
            def _(pe):
                def turn_x(b, first):
                    pe.wait_ge(norm_done, 2 * b + 2)
                    if not first:
                        pe.wait_ge(x2T_copied, b - 1)
                    else:
                        if b == 1:
                            pe.wait_ge(vblock_done, NC)
                    for c in range(DC):
                        for t in range(QT):
                            mm = pe.transpose(ps_misc[:, c * SQ + t * P:c * SQ + (t + 1) * P], xn[:, t, c * P:(c + 1) * P], ident[:])
                    mm.then_inc(xT_done, 1)

                def project_q(b, first):
                    pe.wait_ge(xT_copied, b + 1)
                    if not first:
                        pe.wait_ge(lg_copied, b - 1)
                    for g in range(DC):
                        for c in range(DC):
                            mm = pe.matmul(ps_misc[:, g * SQ:(g + 1) * SQ], wqs[:, c, g * P:(g + 1) * P], xnT[:, c, :],
                                           start=(c == 0), stop=(c == DC - 1))
                    mm.then_inc(q_done, 1)

                def spread_v(b):
                    pe.wait_ge(q_copied, 2 * b + 2)
                    for c in range(NC):
                        c0 = HEAD0[c] * DH
                        mm = pe.matmul(ps_misc[0:ROWS[c], c * 2 * VW:(c + 1) * 2 * VW].rearrange("p (g n) -> p g n", g=DC)[:, :, 0:WIDTH[c]],
                                       spread[:, c * P:c * P + ROWS[c]],
                                       vals[:, bass.ds(b, 1), :].rearrange("p o (g n) -> p (o g) n", g=DC)[:, :, c0:c0 + WIDTH[c]],
                                       start=True, stop=True)
                    mm.then_inc(vspread_done, 1)

                def scores(b, s, first):
                    g, t = s // QT, s % QT
                    if s == 0:
                        pe.wait_ge(q_copied, 2 * b + 2)
                    if t == 0:
                        pe.wait_ge(kblock_done, 2 * b + g + 1)
                    if not (first and s < 2):
                        pe.wait_ge(masked, 2 * (NS * b + s - 1))
                    for h in range(2):
                        mm = pe.matmul(ps_scores[s % 2][:, h, 0:BK], qT[:, g, t * P:(t + 1) * P],
                                       kblock[:, g, 4 * h:4 * h + 4].rearrange("p h k -> p (h k)"), start=True, stop=True)
                    mm.then_inc(scores_done, 1)

                def turn_p(b, s, first):
                    pe.wait_ge(exp_done, NS * b + s + 1)
                    if not (first and s == 0):
                        pe.wait_ge(turned_copied, 2 * (NS * b + s))
                    for c in range(NC):
                        o = ps_probT[0:ROWS[c], c // 4, (c % 4) * P:(c % 4 + 1) * P]
                        mm = pe.transpose(o, prob[:, s % 2, c * P:c * P + ROWS[c]], ident[:])
                    mm.then_inc(turned, 1)

                def attend(b, g, first):
                    pe.wait_ge(turned_copied, 2 * (NS * b + QT * (g + 1)))
                    if not (first and g == 0):
                        pe.wait_ge(av_copied, 2 * b + g)
                    if g == 0:
                        pe.wait_ge(vblock_done, NC * (b + 1))
                    for c in range(NC):
                        pe.matmul(ps_av[:, 0, :], vblock[0:ROWS[c], c, g, :], probT[0:ROWS[c], g, c, :], start=(c == 0), stop=(c == NC - 1))
                    for c in range(NC):
                        mm = pe.matmul(ps_av[:, 1, :], owner[0:ROWS[c], c, :], probT[0:ROWS[c], g, c, :], start=(c == 0), stop=(c == NC - 1))
                    mm.then_inc(av_done, 1)

                def project_o(b, last):
                    pe.wait_ge(av_copied, 2 * b + 2)
                    if last:
                        pe.wait_ge(lg_copied, b)
                    else:
                        pe.wait_ge(vblock_done, NC * (b + 2))
                    for t in range(QT):
                        for g in range(DC):
                            mm = pe.matmul(ps_misc[:, t * D:(t + 1) * D], ctxn[:, g, t * P:(t + 1) * P], wos[:, g, :],
                                           start=(g == 0), stop=(g == DC - 1))
                    mm.then_inc(wo_done, 1)

                def turn_x2(b):
                    pe.wait_ge(norm2_done, 2 * b + 2)
                    for c in range(DC):
                        for t in range(QT):
                            mm = pe.transpose(ps_misc[:, c * SQ + t * P:c * SQ + (t + 1) * P], xn2[:, t, c * P:(c + 1) * P], ident[:])
                    mm.then_inc(x2T_done, 1)

                def route(b, last):
                    pe.wait_ge(x2T_copied, b + 1)
                    if not last:
                        pe.wait_ge(xT_copied, b + 3)
                    for t in range(QT):
                        for c in range(DC):
                            mm = pe.matmul(ps_misc[:, t * E:(t + 1) * E], xn2T[:, c, t * P:(t + 1) * P], rws[:, c, :],
                                           start=(c == 0), stop=(c == DC - 1))
                    mm.then_inc(lg_done, 1)

                def body(b, first=False, last=False):
                    scores(b, 0, first)
                    scores(b, 1, first)
                    if not first:
                        turn_x2(b - 1)
                    turn_p(b, 0, first)
                    scores(b, 2, first)
                    if not last:
                        turn_x(b + 1, first)
                    turn_p(b, 1, first)
                    if not first:
                        route(b - 1, last)
                    scores(b, 3, first)
                    attend(b, 0, first)
                    if not last:
                        project_q(b + 1, first)
                    turn_p(b, 2, first)
                    turn_p(b, 3, first)
                    attend(b, 1, first)
                    if not last:
                        spread_v(b + 1)
                    project_o(b, last)

                pe.wait_ge(ld_first, 16 * 2)
                pe.wait_ge(ld_ctx, LD_CTX)
                for c in range(DC):
                    for b in range(B):
                        mm = pe.transpose(ps_scores[c][:, b // 4, (b % 4) * SK:(b % 4 + 1) * SK], ctxs[:, b, c * P:(c + 1) * P], ident[0:SK, 0:SK])
                    mm.then_inc(ctx_turned, 1)
                pe.wait_ge(ctx_copied, 2)
                for g in range(DC):
                    for h in range(2):
                        for c in range(DC):
                            mm = pe.matmul(ps_scores[g][:, h, 0:4 * SK], wks[:, c, g * P:(g + 1) * P], ctxT[:, c, h * 4 * SK:(h + 1) * 4 * SK],
                                           start=(c == 0), stop=(c == DC - 1))
                    mm.then_inc(keys_done, 1)
                turn_x(0, True)
                for i in range(2):
                    pe.wait_ge(keys_copied, i + 1)
                    for j in range(4):
                        for c in range(DC):
                            mm = pe.matmul(ps_scores[i][0:SK, j // 2, (j % 2) * D:(j % 2 + 1) * D], ctxT[:, c, (4 * i + j) * SK:(4 * i + j + 1) * SK],
                                           wvs[:, c, :], start=(c == 0), stop=(c == DC - 1))
                    mm.then_inc(vals_done, 1)
                pe.wait_ge(ld_rest, 16 * 5)
                project_q(0, True)
                pe.wait_ge(vals_copied, 2)
                spread_v(0)
                body(0, first=True)
                with pe.Fori(1, B - 1) as b:
                    body(b)
                body(B - 1, last=True)
                turn_x2(B - 1)
                route(B - 1, True)
        att.close()
        ffn = ExitStack()
        wb_hi = sb("wb_hi", [P, 3, 2048], F32R, stack=ffn)
        wb_lo = sb("wb_lo", [P, 3, 2048], F32R, stack=ffn)
        act_g = sb("act_g", [P, TC], stack=ffn)
        hid = sb("hid", [P, TC], stack=ffn)
        hid_hi = sb("hid_hi", [P, 2, TC], F32R, stack=ffn)
        hid_lo = sb("hid_lo", [P, 2, TC], F32R, stack=ffn)
        rt_a = sb("rt_a", [P, NT, E, E], stack=ffn)
        rt_b = sb("rt_b", [P, NT, E, E], stack=ffn)
        rt_p = sb("rt_p", [P, NT, E], stack=ffn)
        rt_s = sb("rt_s", [P, NT], stack=ffn)
        ps_g = ffn.enter_context(nc.psum_tensor("ps_g", [P, 2, TC], F32))
        ps_u = ffn.enter_context(nc.psum_tensor("ps_u", [P, 2, TC], F32))
        ps_y = ffn.enter_context(nc.psum_tensor("ps_y", [P, 1, 4, D], F32))
        rt_step, rt_exp = sem("rt_step"), sem("rt_exp")
        up_done, silu_done, hid_done, hid_hi_done, hid_lo_done = sem("up_done"), sem("silu_done"), sem("hid_done"), sem("hid_hi_done"), sem("hid_lo_done")
        y_step, y_added = sem("y_step"), sem("y_added")
        TPC = TC // P
        sets = [[(wa_hi[:, m], wa_lo[:, m]) for m in range(3)],
                [(wb_hi[:, m], wb_lo[:, m]) for m in range(3)]]

        with nc.Block() as block:
            @block.sync
            def _(sp):
                for e in range(1, E):
                    for m in range(3):
                        n = 3 * e + m
                        src = (w1, w3, w2)[m][e].rearrange("(c p) n -> p c n", p=P)
                        sp.wait_ge(w_lo_done, n)
                        sp.dma_start(stage[:].rearrange("p (c n) -> p c n", c=src.shape[1]), src).then_inc(staged, 16)
                for j in range(NTC):
                    sp.wait_ge(y_added, TPC * ((E - 1) * NTC + j + 1))
                    sp.dma_start(out[2 * j:2 * j + 2].rearrange("b (t p) d -> p (b t) d", p=P), xall[:, TPC * j:TPC * (j + 1), :]).then_inc(out_written, 16)
                sp.wait_ge(out_written, 16 * NTC)

            @block.scalar
            def _(act):
                def split(e):
                    for m in range(3):
                        n = 3 * e + m
                        act.wait_ge(staged, 16 * (n + 1))
                        if e >= 2:
                            act.wait_ge(y_step, NTC * FC * (e - 1))
                        act.copy(sets[e % 2][m][0], stage[:]).then_inc(w_hi_done, 1)

                act.wait_ge(rt_step, 2)
                act.activation(rt_p[:], rt_p[:], ACT.Exp).then_inc(rt_exp, 1)
                split(1)
                for e in range(E):
                    with act.Fori(0, NTC) as j:
                        for f in range(FC):
                            n = e * NTC * FC + j * FC + f
                            act.wait_ge(up_done, n + 1)
                            act.wait_ge(hid_done, n)
                            act.activation(act_g[:], ps_g[:, f % 2], ACT.Silu).then_inc(silu_done, 1)
                            act.wait_ge(hid_done, n + 1)
                            if f >= 2:
                                act.wait_ge(y_step, n - 1)
                            else:
                                act.wait_ge(y_step, e * NTC * FC + j * FC)
                            act.copy(hid_hi[:, f % 2], hid[:]).then_inc(hid_hi_done, 1)
                    if e + 2 < E:
                        split(e + 2)

            @block.vector
            def _(dve):
                def split(e):
                    for m in range(3):
                        n = 3 * e + m
                        dve.wait_ge(w_hi_done, n + 1)
                        dve.tensor_tensor(sets[e % 2][m][1], stage[:], sets[e % 2][m][0].bitcast(F32), ALU.subtract).then_inc(w_lo_done, 1)

                steps = [0]

                def link(ins):
                    steps[0] += 1
                    ins.then_inc(rt_step, 1)
                    dve.wait_ge(rt_step, steps[0])

                def over(ap):
                    return ap.unsqueeze(2).to_broadcast([P, NT, E])

                link(dve.tensor_reduce(rt_s[:], logits[:], AX.X, ALU.max))
                link(dve.tensor_tensor(rt_p[:], logits[:], over(rt_s[:]), ALU.subtract))
                dve.wait_ge(rt_exp, 1)
                link(dve.tensor_reduce(rt_s[:], rt_p[:], AX.X, ALU.add))
                link(dve.reciprocal(rt_s[:], rt_s[:]))
                link(dve.tensor_tensor(rt_p[:], rt_p[:], over(rt_s[:]), ALU.mult))
                other = rt_p[:].unsqueeze(2).to_broadcast([P, NT, E, E])
                own = rt_p[:].unsqueeze(3).to_broadcast([P, NT, E, E])
                link(dve.tensor_tensor(rt_a[:], other, own, ALU.is_equal))
                link(dve.tensor_tensor(rt_a[:], rt_a[:], tie[:].unsqueeze(1).to_broadcast([P, NT, E, E]), ALU.mult))
                link(dve.tensor_tensor(rt_b[:], other, own, ALU.is_gt))
                link(dve.tensor_tensor(rt_a[:], rt_a[:], rt_b[:], ALU.add))
                link(dve.tensor_reduce(gates[:], rt_a[:], AX.X, ALU.add))
                link(dve.tensor_scalar(gates[:], gates[:], 2.0, None, ALU.is_lt))
                link(dve.tensor_tensor(gates[:], gates[:], rt_p[:], ALU.mult))
                link(dve.tensor_reduce(rt_s[:], gates[:], AX.X, ALU.add))
                link(dve.reciprocal(rt_s[:], rt_s[:]))
                link(dve.tensor_scalar(rt_s[:], rt_s[:], tanh_g[:, 1:2], None, ALU.mult))
                link(dve.tensor_tensor(gates[:], gates[:], over(rt_s[:]), ALU.mult))
                split(1)

                for e in range(E):
                    with dve.Fori(0, NTC) as j:
                        for f in range(FC):
                            n = e * NTC * FC + j * FC + f
                            dve.wait_ge(silu_done, n + 1)
                            dve.wait_ge(hid_lo_done, n)
                            dve.tensor_tensor(hid[:], act_g[:], ps_u[:, f % 2], ALU.mult).then_inc(hid_done, 1)
                            dve.wait_ge(hid_hi_done, n + 1)
                            dve.tensor_tensor(hid_lo[:, f % 2], hid[:], hid_hi[:, f % 2].bitcast(F32), ALU.subtract).then_inc(hid_lo_done, 1)
                        m = e * NTC + j
                        dve.wait_ge(y_step, FC * (m + 1))
                        dve.wait_ge(y_added, TPC * m)
                        for t in range(TPC):
                            tok = xall[:, bass.ds(j * TPC + t, 1), :].rearrange("p o d -> p (o d)")
                            dve.scalar_tensor_tensor(out=tok, in0=ps_y[:, 0, t], scalar=gates[:, bass.ds(j * TPC + t, 1), e:e + 1].rearrange("p o d -> p (o d)"),
                                                     in1=tok, op0=ALU.mult, op1=ALU.add).then_inc(y_added, 1)
                    if e + 2 < E:
                        split(e + 2)

            @block.tensor
            def _(pe):
                def down(e, j, f):
                    w2h, w2l = (s.rearrange("p (c n) -> p c n", c=FC) for s in sets[e % 2][2])
                    n = e * NTC * FC + j * FC + f
                    pe.wait_ge(hid_lo_done, n + 1)
                    if f == 0:
                        pe.wait_ge(y_added, TPC * (e * NTC + j))
                    for t in range(TPC):
                        hh, hl = (h[:, f % 2, t * P:(t + 1) * P] for h in (hid_hi, hid_lo))
                        for i, (a, w) in enumerate(((hh, w2h), (hh, w2l), (hl, w2h))):
                            mm = pe.matmul(ps_y[:, 0, t], a, w[:, f, :], start=(f == 0 and i == 0 and t % 2 == 0),
                                           stop=(f == FC - 1 and i == 2), skip_group_check=True)
                    mm.then_inc(y_step, 1)

                for e in range(E):
                    pe.wait_ge(w_lo_done, 3 * (e + 1))
                    with pe.Fori(0, NTC) as j:
                        for f in range(FC + 1):
                            if f < FC:
                                n = e * NTC * FC + j * FC + f
                                pe.wait_ge(hid_done, n - 1 if f >= 2 else e * NTC * FC + j * FC)
                                for m, dst in ((0, ps_g), (1, ps_u)):
                                    wh, wl = (s.rearrange("p (c n) -> p c n", c=DC)[:, :, f * P:(f + 1) * P] for s in sets[e % 2][m])
                                    k = 0
                                    for c in range(DC):
                                        xh, xl = (xx[:, c, bass.ds(j * TC, TC)] for xx in (xt_hi, xt_lo))
                                        for a, r in ((wh, xh), (wh, xl), (wl, xh)):
                                            mm = pe.matmul(dst[:, f % 2], a[:, c], r, start=(k == 0), stop=(k == 5))
                                            k += 1
                                mm.then_inc(up_done, 1)
                            if f >= 1:
                                down(e, j, f - 1)
        ffn.close()


LD_CTX = 16 * 14

_CONST = ["ident", "head_rows", "owner", "spread", "tie"]
_INS = ["x", "ctx_1024", "mask_Bx1xSxS2_ff1", "g_xattn", "g_ffn", "L0_xattn_wq_w", "L0_xattn_wq_b", "L0_xattn_wk_w",
        "L0_xattn_wk_b", "L0_xattn_wv_w", "L0_xattn_wv_b", "L0_xattn_wo_w", "L0_xattn_wo_b", "L0_ffn_router_w",
        "L0_ffn_router_b", "L0_ffn_w1", "L0_ffn_w3", "L0_ffn_w2"]


def kernel(**inputs):
    import concourse.bacc as bacc
    from concourse.bass_utils import run_bass_kernel_spmd

    nc = bacc.Bacc("TRN2", target_bir_lowering=False, num_devices=1)
    arrays, args = {}, []
    for name, a in [(n, inputs[n]) for n in _INS] + list(constants().items()):
        a = np.ascontiguousarray(a)
        arrays[f"in_{name}"] = a
        args.append(nc.dram_tensor(f"in_{name}", a.shape, mybir.dt.from_np(a.dtype), kind="ExternalInput").ap())
    result = nc.dram_tensor("out_x", (B, SQ, D), F32, kind="ExternalOutput").ap()
    flamingo_block(nc, *args, result)
    r = run_bass_kernel_spmd(nc, [arrays], core_ids=[0])
    return r.results[0]["out_x"]
```

```python
from contextlib import ExitStack

import numpy as np

import concourse.bass as bass
from concourse import mybir
from concourse.alu_op_type import AluOpType as ALU

ACT = mybir.ActivationFunctionType
F32 = mybir.dt.float32
F32R = mybir.dt.float32r
AX = mybir.AxisListType

P = 128
B, SQ, D = 8, 256, 256
SK = 77
H, DH = 16, 16
E, F = 4, 1024
T = B * SQ
NT = T // P
QT = SQ // P
DC = D // P
HG = H // DC
GK = HG * SK
BK = 4 * SK
NC = -(-GK // P)
ROWS = [min(P, GK - c * P) for c in range(NC)]
HEAD0 = [c * P // SK for c in range(NC)]
VH = DH + 1
WIDTH = [((c * P + ROWS[c] - 1) // SK - HEAD0[c] + 1) * VH for c in range(NC)]
VC = max(WIDTH)
NS = 2 * QT
FC = F // P
TC = 512
NTC = T // TC
WN = (2 * DC * F + FC * D)
PW = 512
NPC = WN // PW
MASKED = -1e9 * 4.0
EPS = 1e-5


def constants():
    row = np.arange(NC * P)
    ident = np.eye(P, dtype=np.float32)
    head_rows = (np.arange(P)[:, None] // DH == np.arange(HG)[None]).astype(np.float32)
    owner = np.zeros((P, NC, VC), np.float32)
    for c in range(NC):
        rows, cols = c * P + np.arange(ROWS[c])[:, None], HEAD0[c] * VH + np.arange(WIDTH[c])[None]
        owner[:ROWS[c], c, :WIDTH[c]] = rows // SK == cols // VH
    spread = (row[None] % SK == np.arange(SK)[:, None]).astype(np.float32)
    tie = (np.arange(E)[None, :] < np.arange(E)[:, None]).astype(np.float32).reshape(1, E * E)
    tie = np.repeat(tie, P, 0)
    return {"ident": ident, "head_rows": head_rows, "owner": owner.reshape(P, NC * VC), "spread": spread, "tie": tie}


def flamingo_block(nc, x, ctx_in, mask, g_xattn, g_ffn, wq, bq, wk, bk, wv, bv, wo, bo,
                   rw, rb, w1, w3, w2, ident_in, head_rows_in, owner_in, spread_in, tie_in, out):
    with ExitStack() as keep:
        def sb(name, shape, dt=F32, stack=keep):
            return stack.enter_context(nc.sbuf_tensor(name, shape, dt))

        def sem(name):
            return keep.enter_context(nc.semaphore(name))

        xall = sb("xall", [P, NT, D])
        logits = sb("logits", [P, NT, E])
        gates = sb("gates", [P, NT, E])
        xt_hi = sb("xt_hi", [P, DC, T], F32R)
        xt_lo = sb("xt_lo", [P, DC, T], F32R)
        wa_hi = sb("wa_hi", [P, WN], F32R)
        wa_lo = sb("wa_lo", [P, WN], F32R)
        stage = sb("stage", [P, 4, PW])
        tanh_g = sb("tanh_g", [P, 2])
        gate_in = sb("gate_in", [P, 2])
        rbias = sb("rbias", [P, E])
        tie = sb("tie", [P, E, E])

        att = ExitStack()
        maskt = sb("maskt", [P, NT, SK], stack=att)
        ctxs = sb("ctxs", [SK, B, D], stack=att)
        ctxT = sb("ctxT", [P, DC, B * SK], stack=att)
        kT = sb("kT", [P, DC, B * SK], stack=att)
        vals = sb("vals", [SK, B, H * VH], stack=att)
        wqs = sb("wqs", [P, DC, D], stack=att)
        wks = sb("wks", [P, DC, D], stack=att)
        wvs = sb("wvs", [P, DC, D], stack=att)
        wos = sb("wos", [P, DC, D], stack=att)
        rws = sb("rws", [P, DC, E], stack=att)
        bqs = sb("bqs", [P, DC], stack=att)
        bks = sb("bks", [P, DC], stack=att)
        bvs = sb("bvs", [P, D], stack=att)
        bos = sb("bos", [P, D], stack=att)
        ident = sb("ident", [P, P], stack=att)
        head_rows = sb("head_rows", [P, HG], stack=att)
        owner = sb("owner", [P, NC, VC], stack=att)
        spread = sb("spread", [SK, NC * P], stack=att)
        half = sb("half", [P, NT], stack=att)
        stats1 = sb("stats1", [P, NT, 6], stack=att)
        mv1 = sb("mv1", [P, NT, 2], stack=att)
        vareps1 = sb("vareps1", [P, NT], stack=att)
        rstd1 = sb("rstd1", [P, NT], stack=att)
        stats = sb("stats", [P, QT, 6], stack=att)
        mv = sb("mv", [P, QT, 2], stack=att)
        vareps = sb("vareps", [P, QT], stack=att)
        rstd = sb("rstd", [P, QT], stack=att)
        xn = sb("xn", [P, QT, D], stack=att)
        xn2 = sb("xn2", [P, QT, D], stack=att)
        xnT = sb("xnT", [P, DC, SQ], stack=att)
        xn2T = sb("xn2T", [P, DC, SQ], stack=att)
        qT = sb("qT", [P, DC, SQ], stack=att)
        kblock = sb("kblock", [P, DC, HG, SK], stack=att)
        vblock = sb("vblock", [P, NC, B, DC, VC], stack=att)
        score = sb("score", [P, 2, HG, SK], stack=att)
        zero_at = sb("zero_at", [P, HG, SK], stack=att)
        top = sb("top", [P, HG], stack=att)
        shift = sb("shift", [P, 2, HG], stack=att)
        prob = sb("prob", [P, 2, HG * SK], stack=att)
        probT = sb("probT", [P, 2, NC, P], stack=att)
        rden = sb("rden", [P, HG], stack=att)
        ctxn = sb("ctxn", [P, QT, H, DH], stack=att)
        ctxnT = sb("ctxnT", [P, DC, SQ], stack=att)

        ps_scores = [att.enter_context(nc.psum_tensor(f"ps_scores{i}", [P, 2, 512], F32)) for i in range(2)]
        ps_probT = att.enter_context(nc.psum_tensor("ps_probT", [P, 2, 512], F32))
        ps_av = att.enter_context(nc.psum_tensor("ps_av", [P, HG, VH], F32))
        ps_misc = att.enter_context(nc.psum_tensor("ps_misc", [P, 512], F32))

        ld_first = sem("ld_first")
        ld_ctx = sem("ld_ctx")
        ld_rest = sem("ld_rest")
        cleared = sem("cleared")
        ctx_turned, ctx_copied = sem("ctx_turned"), sem("ctx_copied")
        keys_done, keys_copied = sem("keys_done"), sem("keys_copied")
        vals_done, vals_copied = sem("vals_done"), sem("vals_copied")
        bo_ready = sem("bo_ready")
        tanh_done = sem("tanh_done")
        stat_step, aggr_step, stat_done, rstd_done, norm_done = sem("stat_step"), sem("aggr_step"), sem("stat_done"), sem("rstd_done"), sem("norm_done")
        stat2_step, aggr2_step, stat2_done, rstd2_done, norm2_done = sem("stat2_step"), sem("aggr2_step"), sem("stat2_done"), sem("rstd2_done"), sem("norm2_done")
        xT_done, xT_copied = sem("xT_done"), sem("xT_copied")
        q_done, q_copied = sem("q_done"), sem("q_copied")
        kblock_done = sem("kblock_done")
        vspread_done, vblock_done = sem("vspread_done"), sem("vblock_done")
        ctxT_done, ctxT_copied = sem("ctxT_done"), sem("ctxT_copied")
        biased = sem("biased")
        scores_done, masked, soft_step, shifted = sem("scores_done"), sem("masked"), sem("soft_step"), sem("shifted")
        exp_done, turned, turned_copied = sem("exp_done"), sem("turned"), sem("turned_copied")
        av_done, rden_done, av_copied = sem("av_done"), sem("rden_done"), sem("av_copied")
        wo_done, x2_done = sem("wo_done"), sem("x2_done")
        x2T_done, x2T_copied = sem("x2T_done"), sem("x2T_copied")
        xhi_done, xlo_done = sem("xhi_done"), sem("xlo_done")
        lg_done, lg_copied = sem("lg_done"), sem("lg_copied")
        staged = [sem(f"staged{i}") for i in range(4)]
        w_hi_done = [sem(f"w_hi_done{i}") for i in range(4)]
        w_lo_done = [sem(f"w_lo_done{i}") for i in range(4)]
        out_written = sem("out_written")

        def piece(e, k):
            m, q = divmod(k, 4)
            if m < 2:
                c, h = divmod(q, 2)
                return (w1, w3)[m][e:e + 1, c * P:(c + 1) * P, h * PW:(h + 1) * PW].rearrange("o p n -> p o n")
            return w2[e, 2 * q * P:2 * (q + 1) * P, :].rearrange("(c p) n -> p c n", p=P)

        def load_piece(eng, e, k, place):
            src = piece(e, k)
            eng.dma_start(stage[:, place].rearrange("p (c n) -> p c n", c=src.shape[1]), src).then_inc(staged[place], 16)

        def wide(ap, n):
            return ap.unsqueeze(1).to_broadcast([ap.shape[0], n, ap.shape[1]])

        with nc.Block() as block:
            @block.sync
            def _(sp):
                for dst, src in ((xall[:, 0:QT, :], x[0:1].rearrange("b (t p) d -> p (b t) d", p=P)),
                                 (ident[:], ident_in)):
                    sp.dma_start(dst, src).then_inc(ld_first, 16)
                for dst, src in ((ctxs[:], ctx_in.rearrange("b k d -> k b d")),
                                 (wks[:], wk.rearrange("(c p) n -> p c n", p=P)),
                                 (wvs[:], wv.rearrange("(c p) n -> p c n", p=P))):
                    sp.dma_start(dst, src).then_inc(ld_ctx, 16)
                for dst, src in ((maskt[:], mask.rearrange("b o (t p) k -> p (b o t) k", p=P)),
                                 (xall[:, QT:, :], x[1:].rearrange("b (t p) d -> p (b t) d", p=P)),
                                 (wqs[:], wq.rearrange("(c p) n -> p c n", p=P)),
                                 (wos[:], wo.rearrange("(c p) n -> p c n", p=P)),
                                 (rws[:], rw.rearrange("(c p) n -> p c n", p=P))):
                    sp.dma_start(dst, src).then_inc(ld_rest, 16)
                for k in range(NPC):
                    if k >= 2:
                        sp.wait_ge(w_lo_done[k % 2], k // 2)
                    load_piece(sp, 0, k, k % 2)

            @block.scalar
            def _(act):
                act.dma_start(owner[:], owner_in.rearrange("p (c n) -> p c n", c=NC)).then_inc(ld_ctx, 16)
                act.dma_start(spread[:], spread_in).then_inc(ld_ctx, 16)
                act.dma_start(head_rows[:], head_rows_in).then_inc(ld_ctx, 16)
                with nc.allow_non_contiguous_dma(reason="biases laid along the partitions"):
                    act.dma_start(bqs[:], bq.rearrange("(c p) -> p c", p=P)).then_inc(ld_ctx, 16)
                    act.dma_start(bks[:], bk.rearrange("(c p) -> p c", p=P)).then_inc(ld_ctx, 16)
                for dst, src in ((bvs[:], bv), (bos[:], bo), (rbias[:], rb), (gate_in[:, 0:1], g_xattn), (gate_in[:, 1:2], g_ffn)):
                    act.dma_start(dst, src.unsqueeze(0).to_broadcast([P, src.shape[0]])).then_inc(ld_ctx, 16)
                act.dma_start(tie[:], tie_in.rearrange("p (i j) -> p i j", i=E)).then_inc(ld_ctx, 16)
                act.wait_ge(ld_ctx, LD_CTX)
                act.activation(tanh_g[:], gate_in[:], ACT.Tanh).then_inc(tanh_done, 1)

                for g in range(DC):
                    act.wait_ge(keys_done, g + 1)
                    act.activation(kT[:, g, :].rearrange("p (h n) -> p h n", h=2), ps_scores[g][:, :, 0:4 * SK],
                                   ACT.Identity, bias=bks[:, g:g + 1]).then_inc(keys_copied, 1)

                def xT_copy(b):
                    act.wait_ge(xT_done, b + 1)
                    act.copy(xnT[:].rearrange("p c n -> p (c n)"), ps_misc[:]).then_inc(xT_copied, 1)

                def q_copy(b):
                    act.wait_ge(q_done, b + 1)
                    act.activation(qT[:, 0, :], ps_misc[:, 0:SQ], ACT.Identity, bias=bqs[:, 0:1]).then_inc(q_copied, 1)
                    act.activation(qT[:, 1, :], ps_misc[:, SQ:], ACT.Identity, bias=bqs[:, 1:2]).then_inc(q_copied, 1)

                def exponent(b, s, first):
                    act.wait_ge(shifted, NS * b + s + 1)
                    if not (first and s < 2):
                        act.wait_ge(turned, NS * b + s - 1)
                    for h in range(HG):
                        ex = act.activation(prob[:, s % 2, h * SK:(h + 1) * SK], score[:, s % 2, h], ACT.Exp,
                                            bias=shift[:, s % 2, h:h + 1], scale=0.25)
                    ex.then_inc(exp_done, 1)

                def probT_copy(b, s, first):
                    n = NS * b + s
                    act.wait_ge(turned, n + 1)
                    if not (first and s < 2):
                        act.wait_ge(av_done, n - 1)
                    act.copy(probT[:, s % 2, 0:4], ps_probT[:, 0, :].rearrange("p (c n) -> p c n", c=4)).then_inc(turned_copied, 1)
                    act.copy(probT[0:ROWS[4], s % 2, 4], ps_probT[0:ROWS[4], 1, 0:P]).then_inc(turned_copied, 1)

                def ctxT_copy(b):
                    act.wait_ge(ctxT_done, b + 1)
                    act.copy(ctxnT[:].rearrange("p c n -> p (c n)"), ps_misc[:]).then_inc(ctxT_copied, 1)

                def body(b, first=False, last=False):
                    if not first:
                        exponent(b - 1, 3, False)
                        probT_copy(b - 1, 3, False)
                    exponent(b, 0, first)
                    if not last:
                        xT_copy(b + 1)
                    probT_copy(b, 0, first)
                    if not first:
                        ctxT_copy(b - 1)
                    exponent(b, 1, first)
                    if not last:
                        q_copy(b + 1)
                    probT_copy(b, 1, first)
                    exponent(b, 2, first)
                    probT_copy(b, 2, first)

                def weights_hi(b):
                    for i in range(2):
                        act.wait_ge(staged[i], 16 * b)
                        act.copy(wa_hi[:, bass.ds((b * 2 + i - 2) * PW, PW)], stage[:, i]).then_inc(w_hi_done[i], 1)

                xT_copy(0)
                q_copy(0)
                body(0, first=True)
                body(1)
                weights_hi(1)
                with act.Fori(2, B - 1) as b:
                    body(b)
                    weights_hi(b)
                body(B - 1, last=True)
                exponent(B - 1, 3, False)
                probT_copy(B - 1, 3, False)
                ctxT_copy(B - 1)
                for b in range(B):
                    act.wait_ge(x2T_done, b + 1)
                    if b:
                        act.wait_ge(xlo_done, b)
                        act.wait_ge(lg_done, b)
                    act.copy(xn2T[:].rearrange("p c n -> p (c n)"), ps_scores[b % 2][:, 0]).then_inc(x2T_copied, 1)
                    act.wait_ge(x2T_copied, b + 1)
                    act.copy(xt_hi[:, :, b * SQ:(b + 1) * SQ], xn2T[:]).then_inc(xhi_done, 1)

            @block.gpsimd
            def _(pool):
                pool.memset(half[:], -0.5).then_inc(cleared, 1)
                pool.memset(vals[:], 1.0).then_inc(cleared, 1)

                def rsqrt(i, t0, t1):
                    pool.wait_ge(stat_done, i + 1)
                    pool.tensor_tensor(rstd1[:, t0:t1], vareps1[:, t0:t1], half[:, t0:t1], ALU.pow).then_inc(rstd_done, 1)

                def rsqrt2(b):
                    pool.wait_ge(stat2_done, b + 1)
                    if b:
                        pool.wait_ge(norm2_done, 2 * b)
                    pool.tensor_tensor(rstd[:], vareps[:], half[:, 0:QT], ALU.pow).then_inc(rstd2_done, 1)

                def keys(b, g):
                    if not (isinstance(b, int) and b == 0):
                        pool.wait_ge(scores_done, NS * (b - 1) + QT * (g + 1))
                    pool.tensor_tensor(kblock[:, g], wide(kT[:, g, bass.ds(b * SK, SK)], HG),
                                       head_rows[:].unsqueeze(2).to_broadcast([P, HG, SK]), ALU.mult).then_inc(kblock_done, 1)

                def bias_add(b):
                    pool.wait_ge(norm_done, 2 * b + 2)
                    pool.tensor_tensor(xall[:, bass.ds(b * QT, QT), :], xall[:, bass.ds(b * QT, QT), :], wide(bos[:], QT),
                                       ALU.add).then_inc(biased, 1)

                def body(b, first=False, last=False):
                    if not last:
                        keys(b + 1, 0)
                        bias_add(b + 1)
                        keys(b + 1, 1)

                def weights_lo(b):
                    for i in range(2):
                        cols = bass.ds((b * 2 + i - 2) * PW, PW)
                        pool.wait_ge(w_hi_done[i], b)
                        pool.tensor_tensor(wa_lo[:, cols], stage[:, i], wa_hi[:, cols].bitcast(F32), ALU.subtract).then_inc(w_lo_done[i], 1)

                pool.wait_ge(cleared, 1)
                rsqrt(0, 0, QT)
                pool.wait_ge(keys_copied, 2)
                keys(0, 0)
                keys(0, 1)
                pool.wait_ge(tanh_done, 1)
                pool.tensor_scalar(bos[:], bos[:], tanh_g[:, 0:1], 0.0, ALU.mult, ALU.add).then_inc(bo_ready, 1)
                pool.wait_ge(bo_ready, 1)
                bias_add(0)
                rsqrt(1, QT, NT)
                body(0, first=True)
                body(1)
                weights_lo(1)
                with pool.Fori(2, B - 1) as b:
                    body(b)
                    weights_lo(b)
                for b in range(B):
                    rsqrt2(b)

            @block.vector
            def _(dve):
                def wait_apart(signal, value):
                    dve.wait_ge(ld_first, 16 * 2)
                    dve.wait_ge(signal, value)

                def stats_of_x(t0, t1):
                    for t in range(t0, t1):
                        dve.bn_stats(stats1[:, t], xall[:, t]).then_inc(stat_step, 1)
                    dve.wait_ge(stat_step, t1)
                    for t in range(t0, t1):
                        dve.bn_aggr(mv1[:, t], stats1[:, t]).then_inc(aggr_step, 1)
                    dve.wait_ge(aggr_step, t1)
                    dve.tensor_scalar(vareps1[:, t0:t1], mv1[:, t0:t1, 1], EPS, None, ALU.add).then_inc(stat_done, 1)

                def norm(b):
                    if isinstance(b, int) and b < 2:
                        dve.wait_ge(rstd_done, b + 1)
                    if not (isinstance(b, int) and b == 0):
                        dve.wait_ge(xT_done, b)
                    for t in range(QT):
                        dve.tensor_scalar(xn[:, t], xall[:, bass.ds(b * QT + t, 1), :].rearrange("p o d -> p (o d)"),
                                          mv1[:, bass.ds(b * QT + t, 1), 0], rstd1[:, bass.ds(b * QT + t, 1)], ALU.subtract, ALU.mult).then_inc(norm_done, 1)

                def residual(b):
                    dve.wait_ge(wo_done, b + 1)
                    dve.wait_ge(biased, b + 1)
                    dve.scalar_tensor_tensor(out=xall[:, bass.ds(b * QT, QT), :], in0=ps_misc[:].rearrange("p (t d) -> p t d", t=QT),
                                             scalar=tanh_g[:, 0:1], in1=xall[:, bass.ds(b * QT, QT), :],
                                             op0=ALU.mult, op1=ALU.add).then_inc(x2_done, 1)

                def stat2(b):
                    wait_apart(x2_done, b + 1)
                    for t in range(QT):
                        st = dve.bn_stats(stats[:, t], xall[:, bass.ds(b * QT + t, 1), :].rearrange("p o d -> p (o d)"))
                    st.then_inc(stat2_step, 1)
                    wait_apart(stat2_step, b + 1)
                    for t in range(QT):
                        st = dve.bn_aggr(mv[:, t], stats[:, t])
                    st.then_inc(aggr2_step, 1)
                    dve.wait_ge(aggr2_step, b + 1)
                    if not (isinstance(b, int) and b == 0):
                        dve.wait_ge(rstd2_done, b)
                    dve.tensor_scalar(vareps[:], mv[:, :, 1], EPS, None, ALU.add).then_inc(stat2_done, 1)

                def norm2(b):
                    dve.wait_ge(rstd2_done, b + 1)
                    if not (isinstance(b, int) and b == 0):
                        dve.wait_ge(x2T_done, b)
                    for t in range(QT):
                        dve.tensor_scalar(xn2[:, t], xall[:, bass.ds(b * QT + t, 1), :].rearrange("p o d -> p (o d)"),
                                          mv[:, t, 0:1], rstd[:, t:t + 1], ALU.subtract, ALU.mult).then_inc(norm2_done, 1)

                def softmax(b, s, first):
                    n = NS * b + s
                    t = s % QT
                    sc = score[:, s % 2]
                    dve.wait_ge(scores_done, n + 1)
                    if not (first and s < 2):
                        dve.wait_ge(exp_done, n - 1)
                    mk = maskt[:, bass.ds(b * QT + t, 1), :].unsqueeze(2).to_broadcast([P, 2, 4, SK])
                    dve.tensor_tensor(sc.rearrange("p (a h) k -> p a h k", a=2), ps_scores[s % 2][:, :, 0:BK].rearrange("p a (h k) -> p a h k", h=4),
                                      mk, ALU.mult).then_inc(masked, 1)
                    dve.wait_ge(masked, n + 1)
                    dve.tensor_scalar(zero_at[:], sc, 0.0, MASKED, ALU.is_equal, ALU.mult).then_inc(soft_step, 1)
                    dve.wait_ge(soft_step, 3 * n + 1)
                    dve.tensor_tensor(sc, sc, zero_at[:], ALU.add).then_inc(soft_step, 1)
                    dve.wait_ge(soft_step, 3 * n + 2)
                    dve.tensor_reduce(top[:], sc, AX.X, ALU.max).then_inc(soft_step, 1)
                    dve.wait_ge(soft_step, 3 * n + 3)
                    dve.tensor_scalar(shift[:, s % 2], top[:], -0.25, None, ALU.mult).then_inc(shifted, 1)

                def context(b, s, first):
                    n = NS * b + s
                    g, t = s // QT, s % QT
                    dve.wait_ge(av_done, n + 1)
                    if not (first and s == 0):
                        dve.wait_ge(av_copied, n)
                    dve.reciprocal(rden[:], ps_av[:, :, DH]).then_inc(rden_done, 1)
                    dve.wait_ge(rden_done, n + 1)
                    if not first:
                        dve.wait_ge(ctxT_done, b)
                    dve.tensor_tensor(ctxn[:, t, g * HG:(g + 1) * HG, :], ps_av[:, :, 0:DH],
                                      rden[:].unsqueeze(2).to_broadcast([P, HG, DH]), ALU.mult).then_inc(av_copied, 1)

                def values(c, i):
                    dve.wait_ge(vspread_done, 2 * c + i + 1)
                    n = WIDTH[c]
                    half_b = slice(i * B // 2, (i + 1) * B // 2)
                    dve.tensor_tensor(vblock[0:ROWS[c], c, half_b, :, 0:n].rearrange("p b g n -> p (b g) n"),
                                      ps_scores[c % 2][0:ROWS[c], i, 0:B * n].rearrange("p (a n) -> p a n", n=n),
                                      wide(owner[0:ROWS[c], c, 0:n], B), ALU.mult).then_inc(vblock_done, 1)

                def split2(b):
                    dve.wait_ge(xhi_done, b + 1)
                    dve.tensor_tensor(xt_lo[:, :, b * SQ:(b + 1) * SQ], xn2T[:], xt_hi[:, :, b * SQ:(b + 1) * SQ].bitcast(F32),
                                      ALU.subtract).then_inc(xlo_done, 1)

                def logit(b):
                    dve.wait_ge(lg_done, b + 1)
                    dve.tensor_tensor(logits[:, bass.ds(b * QT, QT), :], ps_scores[b % 2][:, 1, 0:QT * E].rearrange("p (t e) -> p t e", t=QT),
                                      wide(rbias[:], QT), ALU.add).then_inc(lg_copied, 1)

                def body(b, first=False, last=False):
                    if not first:
                        context(b - 1, 2, False)
                    softmax(b, 0, first)
                    if not last:
                        norm(b + 1)
                    if not first:
                        context(b - 1, 3, False)
                    softmax(b, 1, first)
                    context(b, 0, first)
                    softmax(b, 2, first)
                    context(b, 1, first)
                    if not first:
                        residual(b - 1)
                    softmax(b, 3, first)

                dve.wait_ge(ld_first, 16 * 2)
                stats_of_x(0, QT)
                for c in range(DC):
                    dve.wait_ge(ctx_turned, c + 1)
                    dve.tensor_copy(ctxT[:, c, :].rearrange("p (h n) -> p h n", h=2), ps_scores[c][:, :, 0:4 * SK]).then_inc(ctx_copied, 1)
                norm(0)
                for i in range(2):
                    dve.wait_ge(vals_done, i + 1)
                    if i == 0:
                        dve.wait_ge(cleared, 2)
                    for j in range(4):
                        dve.tensor_tensor(vals[:, 4 * i + j, :].rearrange("p (h n) -> p h n", n=VH)[:, :, 0:DH],
                                          ps_scores[i][0:SK, j // 2, (j % 2) * D:(j % 2 + 1) * D].rearrange("p (h n) -> p h n", n=DH),
                                          bvs[0:SK, :].rearrange("p (h n) -> p h n", n=DH), ALU.add).then_inc(vals_copied, 1)
                for c in range(NC):
                    for i in range(2):
                        values(c, i)
                dve.wait_ge(tanh_done, 1)
                dve.wait_ge(ld_rest, 16 * 5)
                stats_of_x(QT, NT)
                body(0, first=True)
                with dve.Fori(1, B - 1) as b:
                    body(b)
                body(B - 1, last=True)
                context(B - 1, 2, False)
                context(B - 1, 3, False)
                residual(B - 1)
                for b in range(B):
                    stat2(b)
                    norm2(b)
                    if b:
                        split2(b - 1)
                        logit(b - 1)
                split2(B - 1)
                logit(B - 1)

            @block.tensor
            def _(pe):
                def turn_x(b, first):
                    pe.wait_ge(norm_done, 2 * b + 2)
                    if not (isinstance(b, int) and b == 0):
                        pe.wait_ge(q_copied, 2 * b)
                    if not first:
                        pe.wait_ge(x2_done, b - 2)
                    for c in range(DC):
                        for t in range(QT):
                            mm = pe.transpose(ps_misc[:, c * SQ + t * P:c * SQ + (t + 1) * P], xn[:, t, c * P:(c + 1) * P], ident[:])
                    mm.then_inc(xT_done, 1)

                def project_q(b, first):
                    pe.wait_ge(xT_copied, b + 1)
                    if not first:
                        pe.wait_ge(ctxT_copied, b - 1)
                    for g in range(DC):
                        for c in range(DC):
                            mm = pe.matmul(ps_misc[:, g * SQ:(g + 1) * SQ], wqs[:, c, g * P:(g + 1) * P], xnT[:, c, :],
                                           start=(c == 0), stop=(c == DC - 1))
                    mm.then_inc(q_done, 1)

                def spread_v(c, i):
                    if c >= 2:
                        pe.wait_ge(vblock_done, 2 * (c - 2) + i + 1)
                    for j in range(B // 2):
                        n = WIDTH[c]
                        mm = pe.matmul(ps_scores[c % 2][0:ROWS[c], i, j * 2 * n:(j + 1) * 2 * n].rearrange("p (g n) -> p g n", g=DC),
                                       spread[:, c * P:c * P + ROWS[c]],
                                       vals[:, i * B // 2 + j, :].rearrange("p (g n) -> p g n", g=DC)[:, :, HEAD0[c] * VH:HEAD0[c] * VH + n],
                                       start=True, stop=True)
                    mm.then_inc(vspread_done, 1)

                def scores(b, s, first):
                    g, t = s // QT, s % QT
                    if s == 0:
                        pe.wait_ge(q_copied, 2 * b + 2)
                    if t == 0:
                        pe.wait_ge(kblock_done, 2 * b + g + 1)
                    if not (first and s < 2):
                        pe.wait_ge(masked, NS * b + s - 1)
                    for h in range(2):
                        mm = pe.matmul(ps_scores[s % 2][:, h, 0:BK], qT[:, g, t * P:(t + 1) * P],
                                       kblock[:, g, 4 * h:4 * h + 4].rearrange("p h k -> p (h k)"), start=True, stop=True)
                    mm.then_inc(scores_done, 1)

                def turn_p(b, s, first):
                    pe.wait_ge(exp_done, NS * b + s + 1)
                    if not (first and s == 0):
                        pe.wait_ge(turned_copied, 2 * (NS * b + s))
                    for c in range(NC):
                        o = ps_probT[0:ROWS[c], c // 4, (c % 4) * P:(c % 4 + 1) * P]
                        mm = pe.transpose(o, prob[:, s % 2, c * P:c * P + ROWS[c]], ident[:])
                    mm.then_inc(turned, 1)

                def attend(b, s, first):
                    n, g = NS * b + s, s // QT
                    pe.wait_ge(turned_copied, 2 * (n + 1))
                    if not (first and s == 0):
                        pe.wait_ge(av_copied, n)
                    for c in range(NC):
                        w = WIDTH[c]
                        mm = pe.matmul(ps_av[:].rearrange("p h n -> p (h n)")[:, HEAD0[c] * VH:HEAD0[c] * VH + w], probT[0:ROWS[c], s % 2, c, :],
                                       vblock[0:ROWS[c], c, bass.ds(b, 1), g, 0:w].rearrange("p o n -> p (o n)"),
                                       start=(c == 0), stop=(c == NC - 1), skip_group_check=True)
                    mm.then_inc(av_done, 1)

                def turn_ctx(b, last):
                    pe.wait_ge(av_copied, NS * (b + 1))
                    if last:
                        pe.wait_ge(x2_done, b)
                    else:
                        pe.wait_ge(xT_copied, b + 3)
                    for g in range(DC):
                        for t in range(QT):
                            mm = pe.transpose(ps_misc[:, g * SQ + t * P:g * SQ + (t + 1) * P],
                                              ctxn[:, t, g * HG:(g + 1) * HG, :].rearrange("p h n -> p (h n)"), ident[:])
                    mm.then_inc(ctxT_done, 1)

                def project_o(b, last):
                    pe.wait_ge(ctxT_copied, b + 1)
                    if not last:
                        pe.wait_ge(q_copied, 2 * (b + 3))
                    for t in range(QT):
                        for g in range(DC):
                            mm = pe.matmul(ps_misc[:, t * D:(t + 1) * D], ctxnT[:, g, t * P:(t + 1) * P], wos[:, g, :],
                                           start=(g == 0), stop=(g == DC - 1))
                    mm.then_inc(wo_done, 1)

                def body(b, first=False, last=False):
                    scores(b, 1, first)
                    if not first:
                        turn_p(b - 1, 3, False)
                        attend(b - 1, 3, False)
                    scores(b, 2, first)
                    if not last:
                        turn_x(b + 1, first)
                    turn_p(b, 0, first)
                    if not first:
                        turn_ctx(b - 1, last)
                    attend(b, 0, first)
                    scores(b, 3, first)
                    if not last:
                        project_q(b + 1, first)
                    turn_p(b, 1, first)
                    if not first:
                        project_o(b - 1, last)
                    attend(b, 1, first)
                    if not last:
                        scores(b + 1, 0, False)
                    turn_p(b, 2, first)
                    attend(b, 2, first)

                pe.wait_ge(ld_first, 16 * 2)
                pe.wait_ge(ld_ctx, LD_CTX)
                for c in range(DC):
                    for b in range(B):
                        mm = pe.transpose(ps_scores[c][:, b // 4, (b % 4) * SK:(b % 4 + 1) * SK], ctxs[:, b, c * P:(c + 1) * P], ident[0:SK, 0:SK])
                    mm.then_inc(ctx_turned, 1)
                pe.wait_ge(ctx_copied, 2)
                for g in range(DC):
                    for h in range(2):
                        for c in range(DC):
                            mm = pe.matmul(ps_scores[g][:, h, 0:4 * SK], wks[:, c, g * P:(g + 1) * P], ctxT[:, c, h * 4 * SK:(h + 1) * 4 * SK],
                                           start=(c == 0), stop=(c == DC - 1))
                    mm.then_inc(keys_done, 1)
                turn_x(0, True)
                for i in range(2):
                    pe.wait_ge(keys_copied, i + 1)
                    for j in range(4):
                        for c in range(DC):
                            mm = pe.matmul(ps_scores[i][0:SK, j // 2, (j % 2) * D:(j % 2 + 1) * D], ctxT[:, c, (4 * i + j) * SK:(4 * i + j + 1) * SK],
                                           wvs[:, c, :], start=(c == 0), stop=(c == DC - 1))
                    mm.then_inc(vals_done, 1)
                pe.wait_ge(ld_rest, 16 * 5)
                project_q(0, True)
                pe.wait_ge(vals_copied, B)
                for c in range(NC):
                    for i in range(2):
                        spread_v(c, i)
                pe.wait_ge(vblock_done, 2 * NC)
                scores(0, 0, True)
                body(0, first=True)
                with pe.Fori(1, B - 1) as b:
                    body(b)
                body(B - 1, last=True)
                turn_p(B - 1, 3, False)
                attend(B - 1, 3, False)
                turn_ctx(B - 1, True)
                project_o(B - 1, True)
                for b in range(B):
                    if True:
                        pe.wait_ge(norm2_done, 2 * b + 2)
                        for c in range(DC):
                            for t in range(QT):
                                mm = pe.transpose(ps_scores[b % 2][:, 0, c * SQ + t * P:c * SQ + (t + 1) * P], xn2[:, t, c * P:(c + 1) * P], ident[:])
                        mm.then_inc(x2T_done, 1)
                        pe.wait_ge(x2T_copied, b + 1)
                        for t in range(QT):
                            for c in range(DC):
                                mm = pe.matmul(ps_scores[b % 2][:, 1, t * E:(t + 1) * E], xn2T[:, c, t * P:(t + 1) * P], rws[:, c, :],
                                               start=(c == 0), stop=(c == DC - 1))
                        mm.then_inc(lg_done, 1)
        att.close()
        ffn = ExitStack()
        wb_hi = sb("wb_hi", [P, WN], F32R, stack=ffn)
        wb_lo = sb("wb_lo", [P, WN], F32R, stack=ffn)
        act_g = sb("act_g", [P, 2, TC], stack=ffn)
        hid = sb("hid", [P, TC], stack=ffn)
        hid_hi = sb("hid_hi", [P, 2, TC], F32R, stack=ffn)
        hid_lo = sb("hid_lo", [P, 2, TC], F32R, stack=ffn)
        rt_a = sb("rt_a", [P, NT, E, E], stack=ffn)
        rt_b = sb("rt_b", [P, NT, E, E], stack=ffn)
        rt_p = sb("rt_p", [P, NT, E], stack=ffn)
        rt_s = sb("rt_s", [P, NT], stack=ffn)
        ps_g = ffn.enter_context(nc.psum_tensor("ps_g", [P, 2, TC], F32))
        ps_u = ffn.enter_context(nc.psum_tensor("ps_u", [P, 2, TC], F32))
        ps_y = ffn.enter_context(nc.psum_tensor("ps_y", [P, TC // P, D], F32))
        rt_step, rt_exp = sem("rt_step"), sem("rt_exp")
        gate_done, up_done, silu_done, hid_done, hid_hi_done, hid_lo_done = sem("gate_done"), sem("up_done"), sem("silu_done"), sem("hid_done"), sem("hid_hi_done"), sem("hid_lo_done")
        y_step, y_added = sem("y_step"), sem("y_added")
        TPC = TC // P
        wsets = ((wa_hi, wa_lo), (wb_hi, wb_lo))
        CF = NTC * FC
        LOADS = NTC - 1

        def w_in(e, m, part):
            return wsets[e % 2][part][:, m * DC * F:(m + 1) * DC * F].rearrange("p (c n) -> p c n", c=DC)

        def w_out(e, part):
            return wsets[e % 2][part][:, 2 * DC * F:].rearrange("p (c n) -> p c n", c=FC)

        def landed(e, j, i):
            return LOADS * e + j + (NPC // 2 if i < 2 else 0)

        with nc.Block() as block:
            @block.sync
            def _(sp):
                for e in range(E - 1):
                    for j in range(1, NTC):
                        for i in range(4):
                            if landed(e, j, i) > 1:
                                sp.wait_ge(w_lo_done[i], landed(e, j, i) - 1)
                            load_piece(sp, e + 1, 4 * (j - 1) + i, i)
                for j in range(NTC):
                    sp.wait_ge(y_added, TPC * ((E - 1) * NTC + j + 1))
                    sp.dma_start(out[2 * j:2 * j + 2].rearrange("b (t p) d -> p (b t) d", p=P), xall[:, TPC * j:TPC * (j + 1), :]).then_inc(out_written, 16)
                sp.wait_ge(out_written, 16 * NTC)

            @block.scalar
            def _(act):
                act.wait_ge(rt_step, 2)
                act.activation(rt_p[:], rt_p[:], ACT.Exp).then_inc(rt_exp, 1)

                def step(e, j, f):
                    n = e * CF + j * FC + f
                    act.wait_ge(gate_done, n + 1)
                    if not (isinstance(n, int) and n < 2):
                        act.wait_ge(hid_done, n - 1)
                    act.activation(act_g[:, f % 2], ps_g[:, f % 2], ACT.Silu).then_inc(silu_done, 1)
                    act.wait_ge(hid_done, n + 1)
                    if not (isinstance(n, int) and n < 2):
                        act.wait_ge(y_step, n - 1)
                    act.copy(hid_hi[:, f % 2], hid[:]).then_inc(hid_hi_done, 1)

                def weights_hi(e, j, i):
                    act.wait_ge(staged[i], 16 * landed(e, j, i))
                    act.copy(wsets[(e + 1) % 2][0][:, bass.ds((4 * (j - 1) + i) * PW, PW)], stage[:, i]).then_inc(w_hi_done[i], 1)

                for e in range(E):
                    for f in range(FC):
                        step(e, 0, f)
                    with act.Fori(1, NTC) as j:
                        for f in range(FC):
                            step(e, j, f)
                            if e + 1 < E and f % 2:
                                weights_hi(e, j, f // 2)

            @block.vector
            def _(dve):
                steps = [0]

                def link(ins):
                    steps[0] += 1
                    ins.then_inc(rt_step, 1)
                    dve.wait_ge(rt_step, steps[0])

                def over(ap):
                    return ap.unsqueeze(2).to_broadcast([P, NT, E])

                link(dve.tensor_reduce(rt_s[:], logits[:], AX.X, ALU.max))
                link(dve.tensor_tensor(rt_p[:], logits[:], over(rt_s[:]), ALU.subtract))
                dve.wait_ge(rt_exp, 1)
                link(dve.tensor_reduce(rt_s[:], rt_p[:], AX.X, ALU.add))
                link(dve.reciprocal(rt_s[:], rt_s[:]))
                link(dve.tensor_tensor(rt_p[:], rt_p[:], over(rt_s[:]), ALU.mult))
                other = rt_p[:].unsqueeze(2).to_broadcast([P, NT, E, E])
                own = rt_p[:].unsqueeze(3).to_broadcast([P, NT, E, E])
                link(dve.tensor_tensor(rt_a[:], other, own, ALU.is_equal))
                link(dve.tensor_tensor(rt_a[:], rt_a[:], tie[:].unsqueeze(1).to_broadcast([P, NT, E, E]), ALU.mult))
                link(dve.tensor_tensor(rt_b[:], other, own, ALU.is_gt))
                link(dve.tensor_tensor(rt_a[:], rt_a[:], rt_b[:], ALU.add))
                link(dve.tensor_reduce(gates[:], rt_a[:], AX.X, ALU.add))
                link(dve.tensor_scalar(gates[:], gates[:], 2.0, None, ALU.is_lt))
                link(dve.tensor_tensor(gates[:], gates[:], rt_p[:], ALU.mult))
                link(dve.tensor_reduce(rt_s[:], gates[:], AX.X, ALU.add))
                link(dve.reciprocal(rt_s[:], rt_s[:]))
                link(dve.tensor_scalar(rt_s[:], rt_s[:], tanh_g[:, 1:2], None, ALU.mult))
                link(dve.tensor_tensor(gates[:], gates[:], over(rt_s[:]), ALU.mult))

                def step(e, j, f):
                    n = e * CF + j * FC + f
                    dve.wait_ge(silu_done, n + 1)
                    dve.wait_ge(up_done, n + 1)
                    if not (isinstance(n, int) and n < 1):
                        dve.wait_ge(hid_lo_done, n)
                    dve.tensor_tensor(hid[:], act_g[:, f % 2], ps_u[:, f % 2], ALU.mult).then_inc(hid_done, 1)
                    dve.wait_ge(hid_hi_done, n + 1)
                    dve.tensor_tensor(hid_lo[:, f % 2], hid[:], hid_hi[:, f % 2].bitcast(F32), ALU.subtract).then_inc(hid_lo_done, 1)

                def add(e, j):
                    dve.wait_ge(y_step, FC * (e * NTC + j + 1))
                    if not (e == 0 and isinstance(j, int) and j == 0):
                        dve.wait_ge(y_added, TPC * (e * NTC + j))
                    for t in range(TPC):
                        tok = xall[:, bass.ds(j * TPC + t, 1), :].rearrange("p o d -> p (o d)")
                        gate = gates[:, bass.ds(j * TPC + t, 1), e:e + 1].rearrange("p o d -> p (o d)")
                        dve.scalar_tensor_tensor(out=tok, in0=ps_y[:, t], scalar=gate, in1=tok, op0=ALU.mult, op1=ALU.add).then_inc(y_added, 1)

                def weights_lo(e, j, i):
                    hi, lo = (w[:, bass.ds((4 * (j - 1) + i) * PW, PW)] for w in wsets[(e + 1) % 2])
                    dve.wait_ge(w_hi_done[i], landed(e, j, i))
                    dve.tensor_tensor(lo, stage[:, i], hi.bitcast(F32), ALU.subtract).then_inc(w_lo_done[i], 1)

                for e in range(E):
                    for f in range(FC):
                        step(e, 0, f)
                        if f == 0 and e:
                            add(e - 1, NTC - 1)
                    with dve.Fori(1, NTC) as j:
                        for f in range(FC):
                            step(e, j, f)
                            if f == 0:
                                add(e, j - 1)
                            if e + 1 < E and f % 2:
                                weights_lo(e, j, f // 2)
                add(E - 1, NTC - 1)

            @block.tensor
            def _(pe):
                def up(e, j, f):
                    n = e * CF + j * FC + f
                    if not (isinstance(n, int) and n < 2):
                        pe.wait_ge(hid_done, n - 1)
                    for m, dst, done in ((0, ps_g, gate_done), (1, ps_u, up_done)):
                        wh, wl = (w_in(e, m, part)[:, :, f * P:(f + 1) * P] for part in range(2))
                        k = 0
                        for c in range(DC):
                            xh, xl = (xx[:, c, bass.ds(j * TC, TC)] for xx in (xt_hi, xt_lo))
                            for a, r in ((wh, xh), (wh, xl), (wl, xh)):
                                mm = pe.matmul(dst[:, f % 2], a[:, c], r, start=(k == 0), stop=(k == 3 * DC - 1))
                                k += 1
                        mm.then_inc(done, 1)

                def down(e, j, f):
                    n = e * CF + j * FC + f
                    pe.wait_ge(hid_lo_done, n + 1)
                    if f == 0 and not (e == 0 and isinstance(j, int) and j == 0):
                        pe.wait_ge(y_added, TPC * (e * NTC + j))
                    for t in range(TPC):
                        hh, hl = (h[:, f % 2, t * P:(t + 1) * P] for h in (hid_hi, hid_lo))
                        for i, (a, w) in enumerate(((hh, w_out(e, 0)), (hh, w_out(e, 1)), (hl, w_out(e, 0)))):
                            mm = pe.matmul(ps_y[:, t], a, w[:, f, :], start=(f == 0 and i == 0 and t % 2 == 0),
                                           stop=(f == FC - 1 and i == 2), skip_group_check=True)
                    mm.then_inc(y_step, 1)

                def wait_weights(e, k):
                    i = k % 4
                    if e:
                        pe.wait_ge(w_lo_done[i], landed(e - 1, k // 4 + 1, i))
                    else:
                        pe.wait_ge(w_lo_done[k % 2], k // 2 + 1)

                for e in range(E):
                    for k in range(NPC - 4, NPC):
                        wait_weights(e, k)
                    for f in range(FC):
                        up(e, 0, f)
                        if f:
                            down(e, 0, f - 1)
                        elif e:
                            down(e - 1, NTC - 1, FC - 1)
                    with pe.Fori(1, NTC) as j:
                        for f in range(FC):
                            up(e, j, f)
                            if f:
                                down(e, j, f - 1)
                            else:
                                down(e, j - 1, FC - 1)
                down(E - 1, NTC - 1, FC - 1)
        ffn.close()


LD_CTX = 16 * 14

_CONST = ["ident", "head_rows", "owner", "spread", "tie"]
_INS = ["x", "ctx_1024", "mask_Bx1xSxS2_ff1", "g_xattn", "g_ffn", "L0_xattn_wq_w", "L0_xattn_wq_b", "L0_xattn_wk_w",
        "L0_xattn_wk_b", "L0_xattn_wv_w", "L0_xattn_wv_b", "L0_xattn_wo_w", "L0_xattn_wo_b", "L0_ffn_router_w",
        "L0_ffn_router_b", "L0_ffn_w1", "L0_ffn_w3", "L0_ffn_w2"]


def kernel(**inputs):
    import concourse.bacc as bacc
    from concourse.bass_utils import run_bass_kernel_spmd

    nc = bacc.Bacc("TRN2", target_bir_lowering=False, num_devices=1)
    arrays, args = {}, []
    for name, a in [(n, inputs[n]) for n in _INS] + list(constants().items()):
        a = np.ascontiguousarray(a)
        arrays[f"in_{name}"] = a
        args.append(nc.dram_tensor(f"in_{name}", a.shape, mybir.dt.from_np(a.dtype), kind="ExternalInput").ap())
    result = nc.dram_tensor("out_x", (B, SQ, D), F32, kind="ExternalOutput").ap()
    flamingo_block(nc, *args, result)
    r = run_bass_kernel_spmd(nc, [arrays], core_ids=[0])
    return r.results[0]["out_x"]
```

```python
from contextlib import ExitStack

import numpy as np

import concourse.bass as bass
from concourse import mybir
from concourse.alu_op_type import AluOpType as ALU

ACT = mybir.ActivationFunctionType
F32 = mybir.dt.float32
F32R = mybir.dt.float32r
AX = mybir.AxisListType

P = 128
B, SQ, D = 8, 256, 256
SK = 77
H, DH = 16, 16
E, F, TOP = 4, 1024, 2
T = B * SQ
NT = T // P
QT = SQ // P
DC = D // P
HG = H // DC
GK = HG * SK
BK = 4 * SK
NC = -(-GK // P)
ROWS = [min(P, GK - c * P) for c in range(NC)]
HEAD0 = [c * P // SK for c in range(NC)]
VH = DH + 1
WIDTH = [((c * P + ROWS[c] - 1) // SK - HEAD0[c] + 1) * VH for c in range(NC)]
VC = max(WIDTH)
NS = 2 * QT
FC = F // P
TC = 512
NTC = T // TC
TPC = TC // P
WN = (2 * DC * F + FC * D)
PW = 512
NPC = WN // PW
X_PARTS = ((0, 1), (1, B // 2), (B // 2, B))
WARM = 14
EARLY = NPC - B
MASKED = 1e9
EPS = 1e-5


def constants():
    row = np.arange(NC * P)
    ident = np.eye(P, dtype=np.float32)
    head_rows = (np.arange(P)[:, None] // DH == np.arange(HG)[None]).astype(np.float32)
    owner = np.zeros((P, NC, VC), np.float32)
    for c in range(NC):
        rows, cols = c * P + np.arange(ROWS[c])[:, None], HEAD0[c] * VH + np.arange(WIDTH[c])[None]
        owner[:ROWS[c], c, :WIDTH[c]] = rows // SK == cols // VH
    spread = (row[None] % SK == np.arange(SK)[:, None]).astype(np.float32)
    tie = (np.arange(E)[None, :] < np.arange(E)[:, None]).astype(np.float32).reshape(1, E * E)
    small = np.concatenate([ident, np.repeat(tie, P, 0)], 1)
    select = np.concatenate([head_rows, owner.reshape(P, NC * VC), np.pad(spread, ((0, P - SK), (0, 0)))], 1)
    return {"small": small, "select": select}


def flamingo_block(nc, x, ctx_t, mask, rows, columns, wq, wk, wv, wo, rw, w1, w3, w2, small_in, select_in, out):
    with ExitStack() as keep:
        def sb(name, shape, dt=F32, stack=keep):
            return stack.enter_context(nc.sbuf_tensor(name, shape, dt))

        def sem(name):
            return keep.enter_context(nc.semaphore(name))

        xall = sb("xall", [P, NT, D])
        logits = sb("logits", [P, TPC, E])
        gates = sb("gates", [P, NT, E])
        xt_hi = sb("xt_hi", [P, DC, T], F32R)
        xt_lo = sb("xt_lo", [P, DC, T], F32R)
        wa_hi = sb("wa_hi", [P, WN], F32R)
        wa_lo = sb("wa_lo", [P, WN], F32R)
        stage = sb("stage", [P, 4, PW])
        tanh_g = sb("tanh_g", [P, 2])
        row_in = sb("row_in", [P, 2 * D + E + 2])
        bvs, bos = row_in[:, 0:D], row_in[:, D:2 * D]
        rbias, gate_in = row_in[:, 2 * D:2 * D + E], row_in[:, 2 * D + E:]
        rws = sb("rws", [P, DC, E])
        small = sb("small", [P, P + E * E])
        ident, tie = small[:, 0:P], small[:, P:].rearrange("p (i j) -> p i j", i=E)
        half = sb("half", [P, NT])
        stats2 = sb("stats2", [P, TPC, 6])
        mv2 = sb("mv2", [P, TPC, 2])
        vareps2 = sb("vareps2", [P, TPC])
        rstd2 = sb("rstd2", [P, TPC])

        att = ExitStack()
        maskt = sb("maskt", [P, NT, SK], stack=att)
        ctxT = sb("ctxT", [P, DC, B * SK], stack=att)
        blank = sb("blank", [P, P], stack=att)
        kT = sb("kT", [P, DC, B * SK], stack=att)
        vals = sb("vals", [SK, B, H * VH], stack=att)
        wqs = sb("wqs", [P, DC, D], stack=att)
        wks = sb("wks", [P, DC, D], stack=att)
        wvs = sb("wvs", [P, DC, D], stack=att)
        wos = sb("wos", [P, DC, D], stack=att)
        column_in = sb("column_in", [P, 2, DC], stack=att)
        bqs, bks = column_in[:, 0], column_in[:, 1]
        select = sb("select", [P, HG + NC * VC + NC * P], stack=att)
        head_rows = select[:, 0:HG]
        owner = select[:, HG:HG + NC * VC].rearrange("p (c n) -> p c n", c=NC)
        spread = select[0:SK, HG + NC * VC:]
        stats1 = sb("stats1", [P, NT, 6], stack=att)
        mv1 = sb("mv1", [P, NT, 2], stack=att)
        vareps1 = sb("vareps1", [P, NT], stack=att)
        rstd1 = sb("rstd1", [P, NT], stack=att)
        mean_off = sb("mean_off", [P, NT], stack=att)
        xn = sb("xn", [P, QT, D], stack=att)
        xnT = sb("xnT", [P, DC, SQ], stack=att)
        qT = sb("qT", [P, DC, SQ], stack=att)
        kblock = sb("kblock", [P, DC, HG, SK], stack=att)
        vblock = sb("vblock", [P, NC, B, DC, VC], stack=att)
        score = sb("score", [P, NS, HG, SK], stack=att)
        zero_at = sb("zero_at", [P, HG, SK], stack=att)
        lowest = sb("lowest", [P, NS, HG], stack=att)
        prob = sb("prob", [P, 2, HG * SK], stack=att)
        probT = sb("probT", [P, 2, NC, P], stack=att)
        rden = sb("rden", [P, HG], stack=att)
        av = sb("av", [P, 2, HG, VH], stack=att)
        ctxn = sb("ctxn", [P, QT, H, DH], stack=att)
        ctxnT = sb("ctxnT", [P, DC, SQ], stack=att)

        early_xn2 = ctxT[:].rearrange("p c n -> p (c n)")[:, 0:TPC * D].rearrange("p (t d) -> p t d", t=TPC)
        early_xn2T = kT[:].rearrange("p c n -> p (c n)")[:, 0:DC * TC].rearrange("p (c n) -> p c n", c=DC)

        ps_scores = [att.enter_context(nc.psum_tensor(f"ps_scores{i}", [P, 2, 512], F32)) for i in range(2)]
        ps_probT = att.enter_context(nc.psum_tensor("ps_probT", [P, 2, 512], F32))
        ps_av = att.enter_context(nc.psum_tensor("ps_av", [P, HG, VH], F32))
        ps_misc = att.enter_context(nc.psum_tensor("ps_misc", [P, 512], F32))

        ld_x = [sem(f"ld_x{i}") for i in range(len(X_PARTS))]
        ld_small, ld_select, ld_rows, ld_columns, ld_mask = sem("ld_small"), sem("ld_select"), sem("ld_rows"), sem("ld_columns"), sem("ld_mask")
        ld_ctx, ld_wk, ld_wv, ld_wq, ld_wo, ld_rw = sem("ld_ctx"), sem("ld_wk"), sem("ld_wv"), sem("ld_wq"), sem("ld_wo"), sem("ld_rw")
        cleared = sem("cleared")
        mean_off_done = sem("mean_off_done")
        mask_ready = sem("mask_ready")
        keys_done, keys_copied = sem("keys_done"), sem("keys_copied")
        vals_done, vals_copied = sem("vals_done"), sem("vals_copied")
        bo_ready = sem("bo_ready")
        tanh_done = sem("tanh_done")
        stat_step, aggr_step, stat_done, rstd_done, norm_done = sem("stat_step"), sem("aggr_step"), sem("stat_done"), sem("rstd_done"), sem("norm_done")
        stat2_step, aggr2_step, stat2_done, rstd2_done, norm2_done = sem("stat2_step"), sem("aggr2_step"), sem("stat2_done"), sem("rstd2_done"), sem("norm2_done")
        xT_done, xT_copied = sem("xT_done"), sem("xT_copied")
        q_done, q_copied = sem("q_done"), sem("q_copied")
        kblock_done = sem("kblock_done")
        vspread_done, vblock_done = sem("vspread_done"), sem("vblock_done")
        ctxT_done, ctxT_copied = sem("ctxT_done"), sem("ctxT_copied")
        biased = sem("biased")
        scores_done, masked, soft_step, lowest_found, lowered = sem("scores_done"), sem("masked"), sem("soft_step"), sem("lowest_found"), sem("lowered")
        exp_done, turned, turned_copied = sem("exp_done"), sem("turned"), sem("turned_copied")
        av_done, rden_done, av_copied, ctx_done = sem("av_done"), sem("rden_done"), sem("av_copied"), sem("ctx_done")
        wo_done, x2_done = sem("wo_done"), sem("x2_done")
        x2T_done, x2T_copied = sem("x2T_done"), sem("x2T_copied")
        xhi_done, xlo_done = sem("xhi_done"), sem("xlo_done")
        lg_done, lg_copied = sem("lg_done"), sem("lg_copied")
        staged = [sem(f"staged{i}") for i in range(4)]
        w_hi_done = [sem(f"w_hi_done{i}") for i in range(4)]
        w_lo_done = [sem(f"w_lo_done{i}") for i in range(4)]
        out_written = sem("out_written")

        def piece(e, k):
            m, q = divmod(k, 4)
            if m < 2:
                c, h = divmod(q, 2)
                return (w1, w3)[m][e:e + 1, c * P:(c + 1) * P, h * PW:(h + 1) * PW].rearrange("o p n -> p o n")
            return w2[e, 2 * q * P:2 * (q + 1) * P, :].rearrange("(c p) n -> p c n", p=P)

        def load_piece(eng, e, k, place):
            src = piece(e, k)
            eng.dma_start(stage[:, place].rearrange("p (c n) -> p c n", c=src.shape[1]), src).then_inc(staged[place], 16)

        def wide(ap, n):
            return ap.unsqueeze(1).to_broadcast([ap.shape[0], n, ap.shape[1]])

        early_banks = [ps_scores[0][:, c] for c in range(DC)]

        def token_tile(i, t):
            return xall[:, bass.ds(i * TPC + t, 1), :].rearrange("p o d -> p (o d)")

        def after_first(i):
            return not (isinstance(i, int) and i == 0)

        def stats_of(dve, i, tiles):
            for t in tiles:
                st = dve.bn_stats(stats2[:, t], token_tile(i, t))
                st.then_inc(stat2_step, 1)

        def variance(dve, i):
            for t in range(TPC):
                st = dve.bn_aggr(mv2[:, t], stats2[:, t])
            st.then_inc(aggr2_step, 1)
            dve.wait_ge(aggr2_step, i + 1)
            dve.tensor_scalar(vareps2[:], mv2[:, :, 1], EPS, None, ALU.add).then_inc(stat2_done, 1)

        def deviation(pool, i):
            pool.wait_ge(stat2_done, i + 1)
            if after_first(i):
                pool.wait_ge(norm2_done, TPC * i)
            pool.tensor_tensor(rstd2[:], vareps2[:], half[:, 0:TPC], ALU.pow).then_inc(rstd2_done, 1)

        def norm2(dve, i, tiles, xn2):
            dve.wait_ge(rstd2_done, i + 1)
            if after_first(i):
                dve.wait_ge(x2T_done, DC * i)
            for t in tiles:
                dve.tensor_scalar(xn2[:, t], token_tile(i, t), mv2[:, t, 0:1], rstd2[:, t:t + 1], ALU.subtract, ALU.mult).then_inc(norm2_done, 1)

        def turn2(pe, i, xn2, banks):
            pe.wait_ge(norm2_done, TPC * (i + 1))
            if after_first(i):
                pe.wait_ge(x2T_copied, DC * i)
                pe.wait_ge(lg_copied, i)
            for c in range(DC):
                for t in range(TPC):
                    mm = pe.transpose(banks[c][:, t * P:(t + 1) * P], xn2[:, t, c * P:(c + 1) * P], ident)
                mm.then_inc(x2T_done, 1)

        def turned2_copy(act, i, xn2T, banks):
            for c in range(DC):
                act.wait_ge(x2T_done, DC * i + c + 1)
                if c == 0 and after_first(i):
                    act.wait_ge(lg_done, i)
                    act.wait_ge(xlo_done, DC * i)
                act.copy(xn2T[:, c], banks[c]).then_inc(x2T_copied, 1)

        def split_hi(act, i, xn2T):
            for c in range(DC):
                act.wait_ge(x2T_copied, DC * i + c + 1)
                act.copy(xt_hi[:, c, bass.ds(i * TC, TC)], xn2T[:, c]).then_inc(xhi_done, 1)

        def split_lo(dve, i, xn2T):
            for c in range(DC):
                dve.wait_ge(xhi_done, DC * i + c + 1)
                dve.tensor_tensor(xt_lo[:, c, bass.ds(i * TC, TC)], xn2T[:, c], xt_hi[:, c, bass.ds(i * TC, TC)].bitcast(F32),
                                  ALU.subtract).then_inc(xlo_done, 1)

        def route_product(pe, i, xn2T, bank):
            pe.wait_ge(x2T_copied, DC * (i + 1))
            for t in range(TPC):
                for c in range(DC):
                    mm = pe.matmul(bank[:, t * E:(t + 1) * E], xn2T[:, c, t * P:(t + 1) * P], rws[:, c, :],
                                   start=(c == 0), stop=(c == DC - 1))
            mm.then_inc(lg_done, 1)

        def logit(dve, i, bank):
            dve.wait_ge(lg_done, i + 1)
            dve.tensor_tensor(logits[:], bank[:, 0:TPC * E].rearrange("p (t e) -> p t e", t=TPC),
                              wide(rbias, TPC), ALU.add).then_inc(lg_copied, 1)

        with nc.Block() as block:
            @block.sync
            def _(sp):
                def matrix(w):
                    return w.rearrange("(c p) n -> p c n", p=P)

                def load_x(i):
                    b0, b1 = X_PARTS[i]
                    sp.dma_start(xall[:, b0 * QT:b1 * QT, :], x[b0:b1].rearrange("b (t p) d -> p (b t) d", p=P)).then_inc(ld_x[i], 16)

                load_x(0)
                sp.dma_start(ctxT[:], matrix(ctx_t)).then_inc(ld_ctx, 16)
                sp.dma_start(wks[:], matrix(wk)).then_inc(ld_wk, 16)
                sp.dma_start(wvs[:], matrix(wv)).then_inc(ld_wv, 16)
                load_x(1)
                sp.dma_start(wqs[:], matrix(wq)).then_inc(ld_wq, 16)
                sp.dma_start(maskt[:], mask.rearrange("b o (t p) k -> p (b o t) k", p=P)).then_inc(ld_mask, 16)
                load_x(2)
                sp.dma_start(wos[:], matrix(wo)).then_inc(ld_wo, 16)
                sp.dma_start(rws[:], matrix(rw)).then_inc(ld_rw, 16)
                for k in range(EARLY):
                    load_piece(sp, 0, k, k)
                for b in range(B):
                    sp.wait_ge(w_lo_done[0], b + 1)
                    load_piece(sp, 0, EARLY + b, 0)

            @block.scalar
            def _(act):
                act.dma_start(small[:], small_in).then_inc(ld_small, 16)
                with nc.allow_non_contiguous_dma(reason="biases laid along the partitions"):
                    act.dma_start(column_in[:].rearrange("p m c -> p (m c)"), columns.rearrange("(m p) -> p m", p=P)).then_inc(ld_columns, 16)
                act.dma_start(row_in[:], rows.unsqueeze(0).to_broadcast([P, rows.shape[0]])).then_inc(ld_rows, 16)
                act.dma_start(select[:], select_in).then_inc(ld_select, 16)

                def norm(b):
                    if isinstance(b, int) and b < 2:
                        act.wait_ge(mean_off_done, b + 1)
                    if after_first(b):
                        act.wait_ge(xT_done, b)
                    for t in range(QT):
                        act.activation(xn[:, t], xall[:, bass.ds(b * QT + t, 1), :].rearrange("p o d -> p (o d)"), ACT.Identity,
                                       bias=mean_off[:, bass.ds(b * QT + t, 1)], scale=rstd1[:, bass.ds(b * QT + t, 1)]).then_inc(norm_done, 1)

                norm(0)
                act.wait_ge(ld_columns, 16)
                for g in range(DC):
                    act.wait_ge(keys_done, g + 1)
                    act.activation(kT[:, g, :].rearrange("p (h n) -> p h n", h=2), ps_scores[g][:, :, 0:4 * SK],
                                   ACT.Identity, bias=bks[:, g:g + 1]).then_inc(keys_copied, 1)

                def xT_copy(b):
                    act.wait_ge(xT_done, b + 1)
                    act.copy(xnT[:].rearrange("p c n -> p (c n)"), ps_misc[:]).then_inc(xT_copied, 1)

                def q_copy(b):
                    act.wait_ge(q_done, b + 1)
                    act.activation(qT[:, 0, :], ps_misc[:, 0:SQ], ACT.Identity, bias=bqs[:, 0:1]).then_inc(q_copied, 1)
                    act.activation(qT[:, 1, :], ps_misc[:, SQ:], ACT.Identity, bias=bqs[:, 1:2]).then_inc(q_copied, 1)

                def exponent(b, s, first):
                    n = NS * b + s
                    act.wait_ge(lowered, n + 1)
                    if not (first and s < 2):
                        act.wait_ge(turned, n - 1)
                    act.activation(prob[:, s % 2], score[:, s].rearrange("p h k -> p (h k)"), ACT.Exp, scale=-1.0).then_inc(exp_done, 1)

                def probT_copy(b, s, first):
                    n = NS * b + s
                    act.wait_ge(turned, n + 1)
                    if not (first and s < 2):
                        act.wait_ge(av_done, n - 1)
                    act.copy(probT[:, s % 2, 0:4], ps_probT[:, 0, :].rearrange("p (c n) -> p c n", c=4)).then_inc(turned_copied, 1)
                    act.copy(probT[0:ROWS[4], s % 2, 4], ps_probT[0:ROWS[4], 1, 0:P]).then_inc(turned_copied, 1)

                def av_copy(b, s, first):
                    n = NS * b + s
                    act.wait_ge(av_done, n + 1)
                    if not (first and s < 2):
                        act.wait_ge(ctx_done, n - 1)
                    act.copy(av[:, s % 2], ps_av[:]).then_inc(av_copied, 1)

                def ctxT_copy(b):
                    act.wait_ge(ctxT_done, b + 1)
                    act.copy(ctxnT[:].rearrange("p c n -> p (c n)"), ps_misc[:]).then_inc(ctxT_copied, 1)

                def body(b, first=False, last=False):
                    if not last:
                        norm(b + 1)
                    if not first:
                        av_copy(b - 1, 2, False)
                        probT_copy(b - 1, 3, False)
                    if not last:
                        xT_copy(b + 1)
                    exponent(b, 1, first)
                    if not first:
                        av_copy(b - 1, 3, False)
                    probT_copy(b, 0, first)
                    if not last:
                        q_copy(b + 1)
                    av_copy(b, 0, first)
                    exponent(b, 2, first)
                    if not first:
                        ctxT_copy(b - 1)
                    probT_copy(b, 1, first)
                    exponent(b, 3, first)
                    weights_hi(b + EARLY, 0, b + 2)
                    av_copy(b, 1, first)
                    probT_copy(b, 2, first)
                    if not last:
                        exponent(b + 1, 0, False)

                def weights_hi(k, place, turn):
                    act.wait_ge(staged[place], 16 * turn)
                    act.copy(wa_hi[:, bass.ds(k * PW, PW)], stage[:, place]).then_inc(w_hi_done[place], 1)

                xT_copy(0)
                act.wait_ge(ld_rows, 16)
                act.activation(tanh_g[:], gate_in, ACT.Tanh).then_inc(tanh_done, 1)
                q_copy(0)
                for k in range(EARLY):
                    weights_hi(k, k, 1)
                exponent(0, 0, True)
                body(0, first=True)
                body(1)
                act.wait_ge(mean_off_done, len(X_PARTS))
                with act.Fori(2, B - 1) as b:
                    body(b)
                body(B - 1, last=True)
                av_copy(B - 1, 2, False)
                probT_copy(B - 1, 3, False)
                turned2_copy(act, 0, early_xn2T, early_banks)
                av_copy(B - 1, 3, False)
                ctxT_copy(B - 1)
                split_hi(act, 0, early_xn2T)

            @block.gpsimd
            def _(pool):
                pool.memset(half[:], -0.5).then_inc(cleared, 1)
                pool.memset(blank[:], 0.0).then_inc(cleared, 1)
                pool.memset(vals[:].rearrange("p b (h n) -> p b h n", n=VH)[:, :, :, DH:], 1.0).then_inc(cleared, 1)

                def rsqrt(i):
                    t0, t1 = (QT * b for b in X_PARTS[i])
                    pool.wait_ge(stat_done, i + 1)
                    pool.tensor_tensor(rstd1[:, t0:t1], vareps1[:, t0:t1], half[:, t0:t1], ALU.pow).then_inc(rstd_done, 1)

                def keys(b, g):
                    if after_first(b):
                        pool.wait_ge(scores_done, NS * (b - 1) + QT * (g + 1))
                    pool.tensor_tensor(kblock[:, g], wide(kT[:, g, bass.ds(b * SK, SK)], HG),
                                       head_rows.unsqueeze(2).to_broadcast([P, HG, SK]), ALU.mult).then_inc(kblock_done, 1)

                def bias_add(b):
                    pool.wait_ge(norm_done, 2 * b + 2)
                    pool.tensor_tensor(xall[:, bass.ds(b * QT, QT), :], xall[:, bass.ds(b * QT, QT), :], wide(bos, QT),
                                       ALU.add).then_inc(biased, 1)

                def lower(b, s):
                    pool.wait_ge(lowest_found, NS * b + s + 1)
                    pool.tensor_tensor(score[:, s], score[:, s], lowest[:, s].unsqueeze(2).to_broadcast([P, HG, SK]),
                                       ALU.subtract).then_inc(lowered, 1)

                def body(b, first=False, last=False):
                    lower(b, 0)
                    if not last:
                        keys(b + 1, 0)
                    lower(b, 1)
                    for k in range(EARLY if first else 0):
                        weights_lo(k, k, 1)
                    lower(b, 2)
                    if isinstance(b, int) and b == 1:
                        rsqrt(2)
                    if not last:
                        bias_add(b + 1)
                    lower(b, 3)
                    if not last:
                        keys(b + 1, 1)
                    weights_lo(b + EARLY, 0, b + 2)

                def weights_lo(k, place, turn):
                    cols = bass.ds(k * PW, PW)
                    pool.wait_ge(w_hi_done[place], turn)
                    pool.tensor_tensor(wa_lo[:, cols], stage[:, place], wa_hi[:, cols].bitcast(F32), ALU.subtract).then_inc(w_lo_done[place], 1)

                pool.wait_ge(cleared, 1)
                rsqrt(0)
                rsqrt(1)
                pool.wait_ge(ld_select, 16)
                pool.wait_ge(keys_copied, 1)
                keys(0, 0)
                pool.wait_ge(ld_mask, 16)
                pool.tensor_scalar(maskt[:], maskt[:], -1.0 / np.sqrt(DH), 0.0, ALU.mult, ALU.add).then_inc(mask_ready, 1)
                pool.wait_ge(keys_copied, 2)
                keys(0, 1)
                pool.wait_ge(tanh_done, 1)
                pool.wait_ge(ld_rows, 16)
                pool.tensor_scalar(bos, bos, tanh_g[:, 0:1], 0.0, ALU.mult, ALU.add).then_inc(bo_ready, 1)
                pool.wait_ge(bo_ready, 1)
                bias_add(0)
                body(0, first=True)
                body(1)
                with pool.Fori(2, B - 1) as b:
                    body(b)
                body(B - 1, last=True)
                deviation(pool, 0)

            @block.vector
            def _(dve):
                def sums(i, t0, t1):
                    dve.wait_ge(ld_x[i], 16)
                    for t in range(t0, t1):
                        dve.bn_stats(stats1[:, t], xall[:, t]).then_inc(stat_step, 1)

                def variance_of_x(i):
                    t0, t1 = (QT * b for b in X_PARTS[i])
                    dve.wait_ge(stat_step, t1)
                    for t in range(t0, t1):
                        dve.bn_aggr(mv1[:, t], stats1[:, t]).then_inc(aggr_step, 1)
                    dve.wait_ge(aggr_step, t1)
                    dve.tensor_scalar(vareps1[:, t0:t1], mv1[:, t0:t1, 1], EPS, None, ALU.add).then_inc(stat_done, 1)

                def off_mean(i):
                    t0, t1 = (QT * b for b in X_PARTS[i])
                    dve.wait_ge(rstd_done, i + 1)
                    dve.scalar_tensor_tensor(out=mean_off[:, t0:t1], in0=mv1[:, t0:t1, 0], scalar=-1.0, in1=rstd1[:, t0:t1],
                                             op0=ALU.mult, op1=ALU.mult).then_inc(mean_off_done, 1)

                def residual(b):
                    dve.wait_ge(wo_done, b + 1)
                    dve.wait_ge(biased, b + 1)
                    dve.scalar_tensor_tensor(out=xall[:, bass.ds(b * QT, QT), :], in0=ps_misc[:].rearrange("p (t d) -> p t d", t=QT),
                                             scalar=tanh_g[:, 0:1], in1=xall[:, bass.ds(b * QT, QT), :],
                                             op0=ALU.mult, op1=ALU.add).then_inc(x2_done, 1)

                def mask_scores(b, s, first):
                    n = NS * b + s
                    dve.wait_ge(scores_done, n + 1)
                    if not first:
                        dve.wait_ge(exp_done, n + 1 - NS)
                    mask_tile = maskt[:, bass.ds(b * QT + s % QT, 1), :].unsqueeze(2).to_broadcast([P, 2, HG // 2, SK])
                    dve.tensor_tensor(score[:, s].rearrange("p (a h) k -> p a h k", a=2),
                                      ps_scores[s % 2][:, :, 0:BK].rearrange("p a (h k) -> p a h k", k=SK),
                                      mask_tile, ALU.mult).then_inc(masked, 1)

                def find_zeros(b, s):
                    dve.wait_ge(masked, NS * b + s + 1)
                    dve.tensor_scalar(zero_at[:], score[:, s], 0.0, MASKED, ALU.is_equal, ALU.mult).then_inc(soft_step, 1)

                def sink_zeros(b, s):
                    dve.wait_ge(soft_step, 2 * (NS * b + s) + 1)
                    dve.tensor_tensor(score[:, s], score[:, s], zero_at[:], ALU.add).then_inc(soft_step, 1)

                def find_lowest(b, s):
                    dve.wait_ge(soft_step, 2 * (NS * b + s) + 2)
                    dve.tensor_reduce(lowest[:, s], score[:, s], AX.X, ALU.min).then_inc(lowest_found, 1)

                def divide(b, s, first):
                    n = NS * b + s
                    dve.wait_ge(av_copied, n + 1)
                    if not (first and s == 0):
                        dve.wait_ge(ctx_done, n)
                    dve.reciprocal(rden[:], av[:, s % 2, :, DH]).then_inc(rden_done, 1)

                def context(b, s):
                    n = NS * b + s
                    g, t = s // QT, s % QT
                    dve.wait_ge(rden_done, n + 1)
                    if after_first(b):
                        dve.wait_ge(ctxT_done, b)
                    dve.tensor_tensor(ctxn[:, t, g * HG:(g + 1) * HG, :], av[:, s % 2, :, 0:DH],
                                      rden[:].unsqueeze(2).to_broadcast([P, HG, DH]), ALU.mult).then_inc(ctx_done, 1)

                def finish(b, s, first):
                    divide(b, s, first)
                    context(b, s)

                def values(c, i):
                    dve.wait_ge(vspread_done, 2 * c + i + 1)
                    n = WIDTH[c]
                    half_b = slice(i * B // 2, (i + 1) * B // 2)
                    dve.tensor_tensor(vblock[0:ROWS[c], c, half_b, :, 0:n].rearrange("p b g n -> p (b g) n"),
                                      ps_probT[0:ROWS[c], i, 0:B * n].rearrange("p (a n) -> p a n", n=n),
                                      wide(owner[0:ROWS[c], c, 0:n], B), ALU.mult).then_inc(vblock_done, 1)

                def body(b):
                    for s in range(NS):
                        mask_scores(b, s, False)
                        if isinstance(b, int) and b == 1:
                            if s < 2:
                                sums(2, NT - 4 + 2 * s, NT - 2 + 2 * s)
                            elif s == 2:
                                variance_of_x(2)
                            else:
                                off_mean(2)
                        find_zeros(b, s)
                        sink_zeros(b, s)
                        find_lowest(b, s)
                        if s < NS - 1:
                            finish(b - 1, s + 1, False)
                        else:
                            finish(b, 0, False)
                        if s == 0 and not (isinstance(b, int) and b == 1):
                            residual(b - 2)

                for i in range(2):
                    sums(i, *(QT * b for b in X_PARTS[i]))
                    variance_of_x(i)
                    off_mean(i)
                dve.wait_ge(cleared, 3)
                dve.wait_ge(ld_rows, 16)
                for i in range(2):
                    dve.wait_ge(vals_done, i + 1)
                    for j in range(4):
                        dve.tensor_tensor(vals[:, 4 * i + j, :].rearrange("p (h n) -> p h n", n=VH)[:, :, 0:DH],
                                          (ps_probT, ps_scores[1])[i][0:SK, j // 2, (j % 2) * D:(j % 2 + 1) * D].rearrange("p (h n) -> p h n", n=DH),
                                          bvs[0:SK, :].rearrange("p (h n) -> p h n", n=DH), ALU.add).then_inc(vals_copied, 1)
                dve.wait_ge(ld_select, 16)
                dve.wait_ge(mask_ready, 1)
                for s in range(2):
                    mask_scores(0, s, True)
                    values(2 * s, 0)
                    find_zeros(0, s)
                    values(2 * s, 1)
                    sink_zeros(0, s)
                    values(2 * s + 1, 0)
                    find_lowest(0, s)
                    values(2 * s + 1, 1)
                values(NC - 1, 0)
                values(NC - 1, 1)
                for s in range(2, NS):
                    mask_scores(0, s, True)
                    t0 = NT - 8 + 2 * (s - 2)
                    sums(2, t0, t0 + 2)
                    find_zeros(0, s)
                    sink_zeros(0, s)
                    find_lowest(0, s)
                finish(0, 0, True)
                body(1)
                with dve.Fori(2, B - 1) as b:
                    body(b)
                body(B - 1)
                stats_of(dve, 0, range(TPC))
                residual(B - 2)
                dve.wait_ge(stat2_step, TPC)
                variance(dve, 0)
                divide(B - 1, 1, False)
                context(B - 1, 1)
                norm2(dve, 0, range(TPC), early_xn2)
                for s in (2, 3):
                    divide(B - 1, s, False)
                    context(B - 1, s)
                split_lo(dve, 0, early_xn2T)
                logit(dve, 0, ps_scores[1][:, 0])
                residual(B - 1)

            @block.tensor
            def _(pe):
                def turn_x(b):
                    pe.wait_ge(norm_done, 2 * b + 2)
                    if after_first(b):
                        pe.wait_ge(q_copied, 2 * b)
                    if not (isinstance(b, int) and b <= 2):
                        pe.wait_ge(x2_done, b - 2)
                    for c in range(DC):
                        for t in range(QT):
                            mm = pe.transpose(ps_misc[:, c * SQ + t * P:c * SQ + (t + 1) * P], xn[:, t, c * P:(c + 1) * P], ident)
                    mm.then_inc(xT_done, 1)

                def project_q(b):
                    pe.wait_ge(xT_copied, b + 1)
                    for g in range(DC):
                        for c in range(DC):
                            mm = pe.matmul(ps_misc[:, g * SQ:(g + 1) * SQ], wqs[:, c, g * P:(g + 1) * P], xnT[:, c, :],
                                           start=(c == 0), stop=(c == DC - 1))
                    mm.then_inc(q_done, 1)

                def spread_v(c, i):
                    if c:
                        pe.wait_ge(vblock_done, 2 * (c - 1) + i + 1)
                    n = WIDTH[c]
                    pe.matmul(ps_probT[0:ROWS[c], i, 0:B * n].rearrange("p (b g n) -> p b g n", g=DC, n=n),
                              spread[:, c * P:c * P + ROWS[c]],
                              vals[:, i * B // 2:(i + 1) * B // 2, :].rearrange("p b (g n) -> p b g n", g=DC)[:, :, :, HEAD0[c] * VH:HEAD0[c] * VH + n],
                              start=True, stop=True).then_inc(vspread_done, 1)

                def scores(b, s, first):
                    g, t = s // QT, s % QT
                    if s == 0:
                        pe.wait_ge(q_copied, 2 * b + 2)
                    if t == 0:
                        pe.wait_ge(kblock_done, 2 * b + g + 1)
                    if not (first and s < 2):
                        pe.wait_ge(masked, NS * b + s - 1)
                    for h in range(2):
                        mm = pe.matmul(ps_scores[s % 2][:, h, 0:BK], qT[:, g, t * P:(t + 1) * P],
                                       kblock[:, g, 4 * h:4 * h + 4].rearrange("p h k -> p (h k)"), start=True, stop=True)
                    mm.then_inc(scores_done, 1)

                def turn_p(b, s, first):
                    pe.wait_ge(exp_done, NS * b + s + 1)
                    if not (first and s == 0):
                        pe.wait_ge(turned_copied, 2 * (NS * b + s))
                    for c in range(NC):
                        o = ps_probT[0:ROWS[c], c // 4, (c % 4) * P:(c % 4 + 1) * P]
                        mm = pe.transpose(o, prob[:, s % 2, c * P:c * P + ROWS[c]], ident)
                    mm.then_inc(turned, 1)

                def attend(b, s, first):
                    n, g = NS * b + s, s // QT
                    pe.wait_ge(turned_copied, 2 * (n + 1))
                    if not (first and s == 0):
                        pe.wait_ge(av_copied, n)
                    for c in range(NC):
                        w = WIDTH[c]
                        mm = pe.matmul(ps_av[:].rearrange("p h n -> p (h n)")[:, HEAD0[c] * VH:HEAD0[c] * VH + w], probT[0:ROWS[c], s % 2, c, :],
                                       vblock[0:ROWS[c], c, bass.ds(b, 1), g, 0:w].rearrange("p o n -> p (o n)"),
                                       start=(c == 0), stop=(c == NC - 1), skip_group_check=True)
                    mm.then_inc(av_done, 1)

                def turn_ctx(b, last):
                    pe.wait_ge(ctx_done, NS * (b + 1))
                    if last:
                        pe.wait_ge(x2_done, b)
                    else:
                        pe.wait_ge(q_copied, 2 * (b + 3))
                    for g in range(DC):
                        for t in range(QT):
                            mm = pe.transpose(ps_misc[:, g * SQ + t * P:g * SQ + (t + 1) * P],
                                              ctxn[:, t, g * HG:(g + 1) * HG, :].rearrange("p h n -> p (h n)"), ident)
                    mm.then_inc(ctxT_done, 1)

                def project_o(b):
                    pe.wait_ge(ctxT_copied, b + 1)
                    for t in range(QT):
                        for g in range(DC):
                            mm = pe.matmul(ps_misc[:, t * D:(t + 1) * D], ctxnT[:, g, t * P:(t + 1) * P], wos[:, g, :],
                                           start=(g == 0), stop=(g == DC - 1))
                    mm.then_inc(wo_done, 1)

                def body(b, first=False, last=False):
                    if not first:
                        turn_p(b - 1, 3, False)
                    scores(b, 2, first)
                    if not last:
                        turn_x(b + 1)
                    if not first:
                        attend(b - 1, 3, False)
                    if first:
                        pe.wait_ge(vblock_done, 2 * NC)
                        pe.wait_ge(ld_wo, 16)
                        pe.wait_ge(ld_rw, 16)
                    turn_p(b, 0, first)
                    scores(b, 3, first)
                    if not last:
                        project_q(b + 1)
                    attend(b, 0, first)
                    if not first:
                        turn_ctx(b - 1, last)
                    turn_p(b, 1, first)
                    if not last:
                        scores(b + 1, 0, False)
                    attend(b, 1, first)
                    if not first:
                        project_o(b - 1)
                    turn_p(b, 2, first)
                    if not last:
                        scores(b + 1, 1, False)
                    attend(b, 2, first)

                pe.wait_ge(cleared, 2)
                for i in range(WARM):
                    pe.matmul(ps_misc[:, 0:P], blank[:], blank[:], start=True, stop=True)
                pe.wait_ge(ld_ctx, 16)
                pe.wait_ge(ld_wk, 16)
                for g in range(DC):
                    for h in range(2):
                        for c in range(DC):
                            mm = pe.matmul(ps_scores[g][:, h, 0:4 * SK], wks[:, c, g * P:(g + 1) * P], ctxT[:, c, h * 4 * SK:(h + 1) * 4 * SK],
                                           start=(c == 0), stop=(c == DC - 1))
                    mm.then_inc(keys_done, 1)
                pe.wait_ge(ld_small, 16)
                turn_x(0)
                pe.wait_ge(ld_wv, 16)
                for i in range(2):
                    if i:
                        pe.wait_ge(keys_copied, 2)
                    for j in range(4):
                        for c in range(DC):
                            mm = pe.matmul((ps_probT, ps_scores[1])[i][0:SK, j // 2, (j % 2) * D:(j % 2 + 1) * D],
                                           ctxT[:, c, (4 * i + j) * SK:(4 * i + j + 1) * SK],
                                           wvs[:, c, :], start=(c == 0), stop=(c == DC - 1))
                    mm.then_inc(vals_done, 1)
                pe.wait_ge(ld_wq, 16)
                project_q(0)
                scores(0, 0, True)
                pe.wait_ge(vals_copied, B)
                pe.wait_ge(ld_select, 16)
                spread_v(0, 0)
                spread_v(0, 1)
                scores(0, 1, True)
                for c in range(1, NC):
                    for i in range(2):
                        spread_v(c, i)
                body(0, first=True)
                body(1)
                with pe.Fori(2, B - 1) as b:
                    body(b)
                body(B - 1, last=True)
                turn_p(B - 1, 3, False)
                turn2(pe, 0, early_xn2, early_banks)
                attend(B - 1, 3, False)
                route_product(pe, 0, early_xn2T, ps_scores[1][:, 0])
                turn_ctx(B - 1, True)
                project_o(B - 1)
        att.close()

        ffn = ExitStack()
        wb_hi = sb("wb_hi", [P, WN], F32R, stack=ffn)
        wb_lo = sb("wb_lo", [P, WN], F32R, stack=ffn)
        act_g = sb("act_g", [P, 2, TC], stack=ffn)
        hid = sb("hid", [P, TC], stack=ffn)
        hid_hi = sb("hid_hi", [P, 2, TC], F32R, stack=ffn)
        hid_lo = sb("hid_lo", [P, 2, TC], F32R, stack=ffn)
        rt_a = sb("rt_a", [P, TPC, E, E], stack=ffn)
        rt_b = sb("rt_b", [P, TPC, E, E], stack=ffn)
        chosen = sb("chosen", [P, TPC, E], stack=ffn)
        rt_p = sb("rt_p", [P, TPC, E], stack=ffn)
        rt_s = sb("rt_s", [P, TPC], stack=ffn)
        euler = sb("euler", [P, TPC * E], stack=ffn)
        xn2 = sb("xn2", [P, TPC, D], stack=ffn)
        xn2T = sb("xn2T", [P, DC, TC], stack=ffn)
        ps_g = ffn.enter_context(nc.psum_tensor("ps_g", [P, 2, TC], F32))
        ps_u = ffn.enter_context(nc.psum_tensor("ps_u", [P, 2, TC], F32))
        ps_x = ffn.enter_context(nc.psum_tensor("ps_x", [P, 2, TC], F32))
        ps_y = ffn.enter_context(nc.psum_tensor("ps_y", [P, TC // P, D], F32))
        rt_step, rt_exp, euler_set = sem("rt_step"), sem("rt_exp"), sem("euler_set")
        x_banks = [ps_x[:, c] for c in range(DC)]
        gate_done, up_done, silu_done, hid_done, hid_hi_done, hid_lo_done = sem("gate_done"), sem("up_done"), sem("silu_done"), sem("hid_done"), sem("hid_hi_done"), sem("hid_lo_done")
        y_step, y_added = sem("y_step"), sem("y_added")
        wsets = ((wa_hi, wa_lo), (wb_hi, wb_lo))
        CF = NTC * FC
        ROUTE = 16
        LOADS = NTC - 1

        def w_in(e, m, part):
            return wsets[e % 2][part][:, m * DC * F:(m + 1) * DC * F].rearrange("p (c n) -> p c n", c=DC)

        def w_out(e, part):
            return wsets[e % 2][part][:, 2 * DC * F:].rearrange("p (c n) -> p c n", c=FC)

        def landed(e, j, i):
            return LOADS * e + j + (B + 1 if i == 0 else 1)

        with nc.Block() as block:
            @block.sync
            def _(sp):
                for e in range(E - 1):
                    for j in range(1, NTC):
                        for i in range(4):
                            sp.wait_ge(w_lo_done[i], landed(e, j, i) - 1)
                            load_piece(sp, e + 1, 4 * (j - 1) + i, i)

                def write(t0, t1):
                    sp.wait_ge(y_added, TPC * (E - 1) * NTC + t1)
                    sp.dma_start(out.rearrange("b (t p) d -> p (b t) d", p=P)[:, t0:t1, :], xall[:, t0:t1, :]).then_inc(out_written, 16)

                for j in range(NTC - 1):
                    write(TPC * j, TPC * (j + 1))
                for t in range(NT - TPC, NT):
                    write(t, t + 1)
                sp.wait_ge(out_written, 16 * (NTC - 1 + TPC))

            @block.scalar
            def _(act):
                def step(e, j, f):
                    n = e * CF + j * FC + f
                    act.wait_ge(gate_done, n + 1)
                    if not (isinstance(n, int) and n < 2):
                        act.wait_ge(hid_done, n - 1)
                    act.activation(act_g[:, f % 2], ps_g[:, f % 2], ACT.Silu).then_inc(silu_done, 1)
                    act.wait_ge(hid_done, n + 1)
                    if not (isinstance(n, int) and n < 2):
                        act.wait_ge(y_step, n - 1)
                    act.copy(hid_hi[:, f % 2], hid[:]).then_inc(hid_hi_done, 1)

                def weights_hi(e, j, i):
                    act.wait_ge(staged[i], 16 * landed(e, j, i))
                    act.copy(wsets[(e + 1) % 2][0][:, bass.ds((4 * (j - 1) + i) * PW, PW)], stage[:, i]).then_inc(w_hi_done[i], 1)

                def body(e, j, last):
                    for f in range(FC):
                        step(e, j, f)
                        if e + 1 < E and after_first(j) and f % 2:
                            weights_hi(e, j, f // 2)
                        if e == 0 and not last:
                            if f == 5:
                                turned2_copy(act, j + 1, xn2T, x_banks)
                            if f == 6:
                                split_hi(act, j + 1, xn2T)

                for e in range(E):
                    body(e, 0, False)
                    if e == 0:
                        with act.Fori(1, NTC - 1) as j:
                            body(e, j, False)
                        body(e, NTC - 1, True)
                    else:
                        with act.Fori(1, NTC) as j:
                            body(e, j, False)

            @block.gpsimd
            def _(pool):
                pool.memset(euler[:], float(np.e)).then_inc(euler_set, 1)
                pool.wait_ge(euler_set, 1)

                def body(j, last):
                    pool.wait_ge(rt_step, ROUTE * j + 2)
                    pool.tensor_tensor(rt_p[:].rearrange("p t e -> p (t e)"), euler[:], rt_p[:].rearrange("p t e -> p (t e)"), ALU.pow).then_inc(rt_exp, 1)
                    if not last:
                        deviation(pool, j + 1)

                body(0, False)
                with pool.Fori(1, NTC - 1) as j:
                    body(j, False)
                body(NTC - 1, True)

            @block.vector
            def _(dve):
                def route(i, f):
                    def over(ap):
                        return ap.unsqueeze(2).to_broadcast([P, TPC, E])

                    other = rt_p[:].unsqueeze(2).to_broadcast([P, TPC, E, E])
                    own = rt_p[:].unsqueeze(3).to_broadcast([P, TPC, E, E])
                    base = ROUTE * i
                    if f == 0:
                        dve.wait_ge(lg_copied, i + 1)
                        if after_first(i):
                            dve.wait_ge(rt_step, base)
                        dve.tensor_reduce(rt_s[:], logits[:], AX.X, ALU.max).then_inc(rt_step, 1)
                        dve.wait_ge(rt_step, base + 1)
                        dve.tensor_tensor(rt_p[:], logits[:], over(rt_s[:]), ALU.subtract).then_inc(rt_step, 1)
                    elif f == 1:
                        dve.wait_ge(rt_exp, i + 1)
                        dve.tensor_reduce(rt_s[:], rt_p[:], AX.X, ALU.add).then_inc(rt_step, 1)
                        dve.wait_ge(rt_step, base + 3)
                        dve.reciprocal(rt_s[:], rt_s[:]).then_inc(rt_step, 1)
                    elif f == 2:
                        dve.wait_ge(rt_step, base + 4)
                        dve.tensor_tensor(rt_p[:], rt_p[:], over(rt_s[:]), ALU.mult).then_inc(rt_step, 1)
                    elif f == 3:
                        dve.wait_ge(rt_step, base + 5)
                        dve.tensor_tensor(rt_a[:], other, own, ALU.is_equal).then_inc(rt_step, 1)
                        dve.wait_ge(rt_step, base + 6)
                        dve.tensor_tensor(rt_a[:], rt_a[:], tie.unsqueeze(1).to_broadcast([P, TPC, E, E]), ALU.mult).then_inc(rt_step, 1)
                    elif f == 4:
                        dve.tensor_tensor(rt_b[:], other, own, ALU.is_gt).then_inc(rt_step, 1)
                        dve.wait_ge(rt_step, base + 8)
                        dve.tensor_tensor(rt_a[:], rt_a[:], rt_b[:], ALU.add).then_inc(rt_step, 1)
                    elif f == 5:
                        dve.wait_ge(rt_step, base + 9)
                        dve.tensor_reduce(chosen[:], rt_a[:], AX.X, ALU.add).then_inc(rt_step, 1)
                        dve.wait_ge(rt_step, base + 10)
                        dve.tensor_scalar(chosen[:], chosen[:], float(TOP), None, ALU.is_lt).then_inc(rt_step, 1)
                        dve.wait_ge(rt_step, base + 11)
                        dve.tensor_tensor(chosen[:], chosen[:], rt_p[:], ALU.mult).then_inc(rt_step, 1)
                    elif f == 6:
                        dve.wait_ge(rt_step, base + 12)
                        dve.tensor_reduce(rt_s[:], chosen[:], AX.X, ALU.add).then_inc(rt_step, 1)
                        dve.wait_ge(rt_step, base + 13)
                        dve.reciprocal(rt_s[:], rt_s[:]).then_inc(rt_step, 1)
                    else:
                        dve.wait_ge(rt_step, base + 14)
                        dve.tensor_scalar(rt_s[:], rt_s[:], tanh_g[:, 1:2], None, ALU.mult).then_inc(rt_step, 1)
                        dve.wait_ge(rt_step, base + 15)
                        dve.tensor_tensor(gates[:, bass.ds(i * TPC, TPC), :], chosen[:], over(rt_s[:]), ALU.mult).then_inc(rt_step, 1)

                def step(e, j, f):
                    n = e * CF + j * FC + f
                    dve.wait_ge(silu_done, n + 1)
                    dve.wait_ge(up_done, n + 1)
                    if not (isinstance(n, int) and n < 1):
                        dve.wait_ge(hid_lo_done, n)
                    dve.tensor_tensor(hid[:], act_g[:, f % 2], ps_u[:, f % 2], ALU.mult).then_inc(hid_done, 1)
                    dve.wait_ge(hid_hi_done, n + 1)
                    dve.tensor_tensor(hid_lo[:, f % 2], hid[:], hid_hi[:, f % 2].bitcast(F32), ALU.subtract).then_inc(hid_lo_done, 1)

                def add(e, j):
                    dve.wait_ge(y_step, FC * (e * NTC + j + 1))
                    if e:
                        dve.wait_ge(y_added, TPC * ((e - 1) * NTC + j + 1))
                    for t in range(TPC):
                        tok = xall[:, bass.ds(j * TPC + t, 1), :].rearrange("p o d -> p (o d)")
                        gate = gates[:, bass.ds(j * TPC + t, 1), e:e + 1].rearrange("p o d -> p (o d)")
                        dve.scalar_tensor_tensor(out=tok, in0=ps_y[:, t], scalar=gate, in1=tok, op0=ALU.mult, op1=ALU.add).then_inc(y_added, 1)

                def weights_lo(e, j, i):
                    hi, lo = (w[:, bass.ds((4 * (j - 1) + i) * PW, PW)] for w in wsets[(e + 1) % 2])
                    dve.wait_ge(w_hi_done[i], landed(e, j, i))
                    dve.tensor_tensor(lo, stage[:, i], hi.bitcast(F32), ALU.subtract).then_inc(w_lo_done[i], 1)

                def body(e, j, last):
                    for f in range(FC):
                        step(e, j, f)
                        if f == 0 and after_first(j):
                            add(e, j - 1)
                        elif f == 0 and e:
                            add(e - 1, NTC - 1)
                        if e + 1 < E and after_first(j) and f % 2:
                            weights_lo(e, j, f // 2)
                        if e == 0:
                            if not last and f in (1, 2):
                                stats_of(dve, j + 1, range(2 * f - 2, 2 * f))
                            if not last and f == 2:
                                dve.wait_ge(stat2_step, TPC * (j + 2))
                            route(j, f)
                            if not last:
                                ahead(j + 1, f)

                def ahead(i, f):
                    if f == 2:
                        variance(dve, i)
                    if f in (3, 4):
                        norm2(dve, i, range(2 * f - 6, 2 * f - 4), xn2)
                    if f == 6:
                        split_lo(dve, i, xn2T)
                    if f == 7:
                        logit(dve, i, x_banks[0])

                for e in range(E):
                    body(e, 0, False)
                    if e == 0:
                        with dve.Fori(1, NTC - 1) as j:
                            body(e, j, False)
                        body(e, NTC - 1, True)
                    else:
                        with dve.Fori(1, NTC) as j:
                            body(e, j, False)
                add(E - 1, NTC - 1)

            @block.tensor
            def _(pe):
                def up(e, j, f):
                    n = e * CF + j * FC + f
                    if not (isinstance(n, int) and n < 2):
                        pe.wait_ge(hid_done, n - 1)
                    for m, dst, done in ((0, ps_g, gate_done), (1, ps_u, up_done)):
                        wh, wl = (w_in(e, m, part)[:, :, f * P:(f + 1) * P] for part in range(2))
                        k = 0
                        for c in range(DC):
                            xh, xl = (xx[:, c, bass.ds(j * TC, TC)] for xx in (xt_hi, xt_lo))
                            for a, r in ((wh, xh), (wh, xl), (wl, xh)):
                                mm = pe.matmul(dst[:, f % 2], a[:, c], r, start=(k == 0), stop=(k == 3 * DC - 1))
                                k += 1
                        mm.then_inc(done, 1)

                def down(e, j, f):
                    n = e * CF + j * FC + f
                    pe.wait_ge(hid_lo_done, n + 1)
                    if f == 0 and not (e == 0 and isinstance(j, int) and j == 0):
                        pe.wait_ge(y_added, TPC * (e * NTC + j))
                    for t in range(TPC):
                        hh, hl = (h[:, f % 2, t * P:(t + 1) * P] for h in (hid_hi, hid_lo))
                        for i, (a, w) in enumerate(((hh, w_out(e, 0)), (hh, w_out(e, 1)), (hl, w_out(e, 0)))):
                            mm = pe.matmul(ps_y[:, t], a, w[:, f, :], start=(f == 0 and i == 0 and t % 2 == 0),
                                           stop=(f == FC - 1 and i == 2), skip_group_check=True)
                    mm.then_inc(y_step, 1)

                def body(e, j, last):
                    if e == 0:
                        pe.wait_ge(xlo_done, DC * (j + 1))
                    for f in range(FC):
                        up(e, j, f)
                        if f:
                            if not after_first(j) and f % 2:
                                wait_weights(e, 8 + (f - 1) // 2)
                            down(e, j, f - 1)
                        elif after_first(j):
                            down(e, j - 1, FC - 1)
                        elif e:
                            down(e - 1, NTC - 1, FC - 1)
                        if e == 0 and not last:
                            if f == 5:
                                turn2(pe, j + 1, xn2, x_banks)
                            if f == 6:
                                route_product(pe, j + 1, xn2T, x_banks[0])

                def wait_weights(e, k):
                    i = k % 4
                    if e:
                        pe.wait_ge(w_lo_done[i], landed(e - 1, k // 4 + 1, i))
                    else:
                        pe.wait_ge(w_lo_done[i], landed(0, 0, i))

                for e in range(E):
                    for k in range(4, 8):
                        wait_weights(e, k)
                    body(e, 0, False)
                    if e == 0:
                        with pe.Fori(1, NTC - 1) as j:
                            body(e, j, False)
                        body(e, NTC - 1, True)
                    else:
                        with pe.Fori(1, NTC) as j:
                            body(e, j, False)
                down(E - 1, NTC - 1, FC - 1)
        ffn.close()


_WEIGHTS = ["L0_xattn_wq_w", "L0_xattn_wk_w", "L0_xattn_wv_w", "L0_xattn_wo_w", "L0_ffn_router_w", "L0_ffn_w1", "L0_ffn_w3", "L0_ffn_w2"]


def kernel(**inputs):
    import concourse.bacc as bacc
    from concourse.bass_utils import run_bass_kernel_spmd

    nc = bacc.Bacc("TRN2", target_bir_lowering=False, num_devices=1)
    arrays, args = {}, []
    laid = {"x": inputs["x"],
            "ctx_t": np.asarray(inputs["ctx_1024"]).transpose(2, 0, 1).reshape(D, B * SK),
            "mask": inputs["mask_Bx1xSxS2_ff1"],
            "rows": np.concatenate([inputs[n] for n in ("L0_xattn_wv_b", "L0_xattn_wo_b", "L0_ffn_router_b", "g_xattn", "g_ffn")]),
            "columns": np.concatenate([inputs[n] for n in ("L0_xattn_wq_b", "L0_xattn_wk_b")])}
    for name, a in list(laid.items()) + [(n, inputs[n]) for n in _WEIGHTS] + list(constants().items()):
        a = np.ascontiguousarray(a)
        arrays[f"in_{name}"] = a
        args.append(nc.dram_tensor(f"in_{name}", a.shape, mybir.dt.from_np(a.dtype), kind="ExternalInput").ap())
    result = nc.dram_tensor("out_x", (B, SQ, D), F32, kind="ExternalOutput").ap()
    flamingo_block(nc, *args, result)
    r = run_bass_kernel_spmd(nc, [arrays], core_ids=[0])
    return r.results[0]["out_x"]
```
